# Optimizing a Trainium2 kernel written in Bass

```python
import numpy as np
import jax
import jax.numpy as jnp

def _softmax(x, axis=-1):
    return jax.nn.softmax(x, axis=axis)

def _gelu(x):
    return jax.nn.gelu(x, approximate=True)

def _silu(x):
    return jax.nn.silu(x)

def _sigmoid(x):
    return jax.nn.sigmoid(x)

def _layernorm(x, axis=-1, eps=1e-05):
    m = jnp.mean(x, axis=axis, keepdims=True)
    v = jnp.var(x, axis=axis, keepdims=True)
    return (x - m) / jnp.sqrt(v + eps)

def _scatter_add(tgt, idx, src, axis=0):
    return tgt.at[idx].add(src)

def _segment_sum(src, seg, n):
    return jax.ops.segment_sum(src, seg, n)
kernel_name = 'mk_flamingo_gated_d2_seqx_r4_0fbf85'

def setup_inputs(seed: int=0):
    np.random.seed(seed)
    _w = jnp.asarray

    def _rec_inputs():
        import jax
        import jax.numpy as jnp
        _rk = jax.random.key(seed)
        x = 7.22e-05 + 1 * jax.random.normal(jax.random.fold_in(_rk, 1), (4, 512, 256), jnp.float32)
        _lenS = 512 - jax.random.randint(jax.random.fold_in(_rk, 7), (4,), 0, max(1, 512 // 4) + 1, jnp.int32)
        _lenS2 = 512 - jax.random.randint(jax.random.fold_in(_rk, 8), (4,), 0, max(1, 512 // 4) + 1, jnp.int32)
        _ctx_1024P = jax.random.normal(jax.random.fold_in(_rk, 11), (4, 16, 256), jnp.float32)
        _ctx_1024c = jax.random.dirichlet(jax.random.fold_in(_rk, 511), 0.3 * jnp.ones((16,), jnp.float32), (4, 512))
        _ctx_1024t = jnp.einsum('bsk,bkd->bsd', _ctx_1024c, _ctx_1024P)
        _ctx_1024t = _ctx_1024t * jax.lax.rsqrt(jnp.mean(jnp.square(_ctx_1024t)) + 1e-12) * 0.953939
        ctx_1024 = 4.13588e-05 + 0.999923 * (_ctx_1024t + 0.3 * jax.random.normal(jax.random.fold_in(_rk, 611), (4, 512, 256), jnp.float32))
        _g = jax.random.normal(jax.random.fold_in(_rk, 9001), (2, 2), jnp.float32)
        _g = jnp.sign(_g) * jnp.maximum(jnp.abs(_g), 1.0) + (_g == 0) * 1.0
        g_xattn = _g[0]
        g_ffn = _g[1]
        return (x, ctx_1024, g_xattn, g_ffn)
    x, ctx_1024, g_xattn, g_ffn = _rec_inputs()

    def _L0_xattn_setup():
        import jax, jax.numpy as jnp
        import numpy as np
        import math
        D_MODEL = 256
        N_HEADS = 16
        D_K = D_MODEL // N_HEADS
        B, L = (4, 512)

        def _heads(x):
            b, l, _ = x.shape
            return x.reshape(b, l, N_HEADS, D_K).transpose(0, 2, 1, 3)
        key = jax.random.key(seed)
        ks = jax.random.split(key, 11)
        s = 1.0 / math.sqrt(D_MODEL)
        inp = {'queries': jax.random.normal(ks[0], (B, L, D_MODEL), jnp.float32), 'keys': jax.random.normal(ks[1], (B, L, D_MODEL), jnp.float32), 'values': jax.random.normal(ks[2], (B, L, D_MODEL), jnp.float32), 'Wq': jax.random.normal(ks[3], (D_MODEL, D_MODEL), jnp.float32) * s, 'bq': jax.random.normal(ks[4], (D_MODEL,), jnp.float32) * s, 'Wk': jax.random.normal(ks[5], (D_MODEL, D_MODEL), jnp.float32) * s, 'bk': jax.random.normal(ks[6], (D_MODEL,), jnp.float32) * s, 'Wv': jax.random.normal(ks[7], (D_MODEL, D_MODEL), jnp.float32) * s, 'bv': jax.random.normal(ks[8], (D_MODEL,), jnp.float32) * s, 'Wo': jax.random.normal(ks[9], (D_MODEL, D_MODEL), jnp.float32) * s, 'bo': jax.random.normal(ks[10], (D_MODEL,), jnp.float32) * s}
        return inp
    _L0_xattn_all = _L0_xattn_setup()
    _L0_xattn_in = {k: v for k, v in _L0_xattn_all.items() if k in ('Wq', 'bq', 'Wk', 'bk', 'Wv', 'bv', 'Wo', 'bo')}
    del _L0_xattn_all

    def _L0_ffn_setup():
        import jax, jax.numpy as jnp
        import numpy as np
        EPS = 1e-05

        def _quantize(W):
            gamma = jnp.mean(jnp.abs(W))
            return jnp.clip(jnp.round(W / (gamma + EPS)), -1.0, 1.0)
        key = jax.random.key(seed)
        k_x, k_w1, k_b1, k_w2, k_b2 = jax.random.split(key, 5)
        n_embd = 256
        d_ff = 4 * n_embd
        B, S = (4, 1024)
        bound1 = 1.0 / np.sqrt(n_embd)
        bound2 = 1.0 / np.sqrt(d_ff)
        x = jax.random.normal(k_x, (B, S, n_embd), dtype=jnp.float32)
        W1 = jax.random.uniform(k_w1, (d_ff, n_embd), jnp.float32, -bound1, bound1)
        b1 = jax.random.uniform(k_b1, (d_ff,), jnp.float32, -bound1, bound1)
        W2 = jax.random.uniform(k_w2, (n_embd, d_ff), jnp.float32, -bound2, bound2)
        b2 = jax.random.uniform(k_b2, (n_embd,), jnp.float32, -bound2, bound2)
        return {'x': x, 'W1': W1, 'b1': b1, 'W2': W2, 'b2': b2}
    _L0_ffn_all = _L0_ffn_setup()
    _L0_ffn_in = {k: v for k, v in _L0_ffn_all.items() if k in ('W1', 'b1', 'W2', 'b2')}
    del _L0_ffn_all

    def _L1_xattn_setup():
        import jax, jax.numpy as jnp
        import numpy as np
        BETA = 256
        NUM_HEADS = 16
        NORM = (BETA // NUM_HEADS) ** (-0.5)
        key = jax.random.key(seed)
        ks = jax.random.split(key, 6)
        B, N = (4, 512)
        D_in_q = D_in_k = D_in_v = 256
        D_out_k = D_out_v = 256
        q = jax.random.normal(ks[0], (B, N, D_in_q), dtype=jnp.float32)
        k = jax.random.normal(ks[1], (B, N, D_in_k), dtype=jnp.float32)
        v = jax.random.normal(ks[2], (B, N, D_in_v), dtype=jnp.float32)
        Wq = jax.random.normal(ks[3], (D_out_k, D_in_q), dtype=jnp.float32) * D_in_q ** (-0.5)
        Wk = jax.random.normal(ks[4], (D_out_k, D_in_k), dtype=jnp.float32) * D_in_k ** (-0.5)
        Wv = jax.random.normal(ks[5], (D_out_v, D_in_v), dtype=jnp.float32) * D_in_v ** (-0.5)
        return {'q': q, 'k': k, 'v': v, 'Wq': Wq, 'Wk': Wk, 'Wv': Wv}
    _L1_xattn_all = _L1_xattn_setup()
    _L1_xattn_in = {k: v for k, v in _L1_xattn_all.items() if k in ('Wq', 'Wk', 'Wv')}
    del _L1_xattn_all

    def _L1_ffn_setup():
        import jax, jax.numpy as jnp
        import numpy as np
        H = 256
        I = 1024
        E = 4
        LN_EPS = 1e-12

        def _layer_norm(x, gamma, beta, eps=LN_EPS):
            mu = jnp.mean(x, axis=-1, keepdims=True)
            var = jnp.mean(jnp.square(x - mu), axis=-1, keepdims=True)
            return (x - mu) * jax.lax.rsqrt(var + eps) * gamma + beta
        key = jax.random.key(seed)
        ks = jax.random.split(key, 8)
        B, S = (4, 128)
        scale = 0.02
        return {'hidden_states': jax.random.normal(ks[0], (B, S, H), jnp.float32), 'W_router': jax.random.normal(ks[1], (H, E), jnp.float32) * scale, 'W1': jax.random.normal(ks[2], (E, H, I), jnp.float32) * scale, 'b1': jax.random.normal(ks[3], (E, I), jnp.float32) * scale, 'Wo': jax.random.normal(ks[4], (I, H), jnp.float32) * scale, 'bo': jax.random.normal(ks[5], (H,), jnp.float32) * scale, 'ln_gamma': jnp.ones((H,), jnp.float32), 'ln_beta': jnp.zeros((H,), jnp.float32)}
    _L1_ffn_all = _L1_ffn_setup()
    _L1_ffn_in = {k: v for k, v in _L1_ffn_all.items() if k in ('W_router', 'W1', 'b1', 'Wo', 'bo', 'ln_gamma', 'ln_beta')}
    del _L1_ffn_all
    return {'x': x, 'ctx_1024': ctx_1024, 'g_xattn': g_xattn, 'g_ffn': g_ffn, 'L0_xattn_Wq': _L0_xattn_in['Wq'], 'L0_xattn_bq': _L0_xattn_in['bq'], 'L0_xattn_Wk': _L0_xattn_in['Wk'], 'L0_xattn_bk': _L0_xattn_in['bk'], 'L0_xattn_Wv': _L0_xattn_in['Wv'], 'L0_xattn_bv': _L0_xattn_in['bv'], 'L0_xattn_Wo': _L0_xattn_in['Wo'], 'L0_xattn_bo': _L0_xattn_in['bo'], 'L0_ffn_W1': _L0_ffn_in['W1'], 'L0_ffn_b1': _L0_ffn_in['b1'], 'L0_ffn_W2': _L0_ffn_in['W2'], 'L0_ffn_b2': _L0_ffn_in['b2'], 'L1_xattn_Wq': _L1_xattn_in['Wq'], 'L1_xattn_Wk': _L1_xattn_in['Wk'], 'L1_xattn_Wv': _L1_xattn_in['Wv'], 'L1_ffn_W_router': _L1_ffn_in['W_router'], 'L1_ffn_W1': _L1_ffn_in['W1'], 'L1_ffn_b1': _L1_ffn_in['b1'], 'L1_ffn_Wo': _L1_ffn_in['Wo'], 'L1_ffn_bo': _L1_ffn_in['bo'], 'L1_ffn_ln_gamma': _L1_ffn_in['ln_gamma'], 'L1_ffn_ln_beta': _L1_ffn_in['ln_beta']}

def reference(x, ctx_1024, g_xattn, g_ffn, L0_xattn_Wq, L0_xattn_bq, L0_xattn_Wk, L0_xattn_bk, L0_xattn_Wv, L0_xattn_bv, L0_xattn_Wo, L0_xattn_bo, L0_ffn_W1, L0_ffn_b1, L0_ffn_W2, L0_ffn_b2, L1_xattn_Wq, L1_xattn_Wk, L1_xattn_Wv, L1_ffn_W_router, L1_ffn_W1, L1_ffn_b1, L1_ffn_Wo, L1_ffn_bo, L1_ffn_ln_gamma, L1_ffn_ln_beta):
    import jax
    import jax.numpy as jnp

    def _L0_xattn_ref(queries, keys, values, Wq, bq, Wk, bk, Wv, bv, Wo, bo):
        import jax, jax.numpy as jnp
        import numpy as np
        import math
        D_MODEL = 256
        N_HEADS = 16
        D_K = D_MODEL // N_HEADS
        B, L = (4, 512)

        def _heads(x):
            b, l, _ = x.shape
            return x.reshape(b, l, N_HEADS, D_K).transpose(0, 2, 1, 3)
        Q = _heads(queries @ Wq.T + bq)
        K = _heads(keys @ Wk.T + bk)
        V = _heads(values @ Wv.T + bv)
        scores = jnp.einsum('bhqd,bhkd->bhqk', Q, K) / math.sqrt(D_K)
        t = jnp.arange(L, dtype=scores.dtype)
        time_bias = -0.1 * jnp.abs(t[None, :] - t[:, None])
        attn = jax.nn.softmax(scores + time_bias[None, None], axis=-1)
        out = jnp.einsum('bhqk,bhkd->bhqd', attn, V)
        out = out.transpose(0, 2, 1, 3).reshape(queries.shape[0], L, D_MODEL)
        return out @ Wo.T + bo

    def _L0_ffn_ref(x, W1, b1, W2, b2):
        import jax, jax.numpy as jnp
        import numpy as np
        EPS = 1e-05

        def _quantize(W):
            gamma = jnp.mean(jnp.abs(W))
            return jnp.clip(jnp.round(W / (gamma + EPS)), -1.0, 1.0)
        Wq1 = _quantize(W1)
        Wq2 = _quantize(W2)
        h = jax.nn.relu(jnp.einsum('bsd,fd->bsf', x, Wq1) + b1)
        out = jnp.einsum('bsf,df->bsd', h, Wq2) + b2
        return out

    def _L1_xattn_ref(q, k, v, Wq, Wk, Wv):
        import jax, jax.numpy as jnp
        import numpy as np
        BETA = 256
        NUM_HEADS = 16
        NORM = (BETA // NUM_HEADS) ** (-0.5)
        qp = jax.nn.relu(jnp.einsum('bnd,od->bno', q, Wq))
        kp = jax.nn.relu(jnp.einsum('bnd,od->bno', k, Wk))
        vp = jax.nn.relu(jnp.einsum('bnd,od->bno', v, Wv))
        B, N, D = qp.shape
        dh = D // NUM_HEADS
        qh = qp.reshape(B, N, NUM_HEADS, dh)
        kh = kp.reshape(B, N, NUM_HEADS, dh)
        vh = vp.reshape(B, N, NUM_HEADS, vp.shape[-1] // NUM_HEADS)
        E = NORM * jnp.einsum('bqhd,bkhd->bhqk', qh, kh)
        A = jax.nn.softmax(E, axis=-1)
        out = jnp.einsum('bhqk,bkhd->bqhd', A, vh)
        return out.reshape(B, N, -1)

    def _L1_ffn_ref(hidden_states, W_router, W1, b1, Wo, bo, ln_gamma, ln_beta):
        import jax, jax.numpy as jnp
        import numpy as np
        H = 256
        I = 1024
        E = 4
        LN_EPS = 1e-12

        def _layer_norm(x, gamma, beta, eps=LN_EPS):
            mu = jnp.mean(x, axis=-1, keepdims=True)
            var = jnp.mean(jnp.square(x - mu), axis=-1, keepdims=True)
            return (x - mu) * jax.lax.rsqrt(var + eps) * gamma + beta
        B, S, _ = hidden_states.shape
        x = hidden_states.reshape(-1, H)
        logits = x @ W_router
        expert_idx = jnp.argmax(logits, axis=-1)
        h = jnp.einsum('th,ehi->tei', x, W1) + b1
        h = jax.nn.gelu(h, approximate=False)
        onehot = jax.nn.one_hot(expert_idx, E, dtype=x.dtype)
        intermediate = jnp.einsum('te,tei->ti', onehot, h)
        y = intermediate @ Wo + bo + x
        y = _layer_norm(y, ln_gamma, ln_beta)
        return y.reshape(B, S, H)
    x = x + jnp.tanh(g_xattn[0]) * _L0_xattn_ref(_layernorm(x, axis=-1), ctx_1024, ctx_1024, L0_xattn_Wq, L0_xattn_bq, L0_xattn_Wk, L0_xattn_bk, L0_xattn_Wv, L0_xattn_bv, L0_xattn_Wo, L0_xattn_bo)
    x = x + jnp.tanh(g_ffn[0]) * _L0_ffn_ref(_layernorm(x, axis=-1), L0_ffn_W1, L0_ffn_b1, L0_ffn_W2, L0_ffn_b2)
    x = x + jnp.tanh(g_xattn[1]) * _L1_xattn_ref(_layernorm(x, axis=-1), ctx_1024, ctx_1024, L1_xattn_Wq, L1_xattn_Wk, L1_xattn_Wv)
    x = x + jnp.tanh(g_ffn[1]) * _L1_ffn_ref(_layernorm(x, axis=-1), L1_ffn_W_router, L1_ffn_W1, L1_ffn_b1, L1_ffn_Wo, L1_ffn_bo, L1_ffn_ln_gamma, L1_ffn_ln_beta)
    return x

_drawn_inputs = setup_inputs


def setup_inputs(seed=0):
    import zlib

    import numpy as np

    out = dict(_drawn_inputs(seed))
    spreads = {'g_ffn': (-1.0, 0.6), 'L1_ffn_ln_gamma': (1.0, 0.6), 'L1_ffn_ln_beta': (0.0, 2.0)}
    factors = {'L0_xattn_bq': 5.359,
     'L0_xattn_bk': 64.0,
     'L0_ffn_b1': 23.049,
     'L0_ffn_b2': 64.0,
     'L1_xattn_Wq': 8.0,
     'L1_xattn_Wk': 8.0,
     'L1_xattn_Wv': 8.0,
     'L1_ffn_W_router': 64.0,
     'L1_ffn_W1': 64.0,
     'L1_ffn_b1': 64.0,
     'L1_ffn_Wo': 64.0,
     'L1_ffn_bo': 64.0}
    for name, (base, spread) in spreads.items():
        noise = np.random.default_rng([zlib.crc32(name.encode()), seed]).standard_normal(out[name].shape)
        drawn = base * np.exp(spread * noise) if base else spread * noise
        out[name] = jnp.asarray(drawn.astype(out[name].dtype))
    for name, factor in factors.items():
        out[name] = (out[name] * factor).astype(out[name].dtype)
    return out
```

```python
from contextlib import ExitStack

import numpy as np
import concourse.bass as bass
from concourse import mybir

ALU = mybir.AluOpType
ACT = mybir.ActivationFunctionType
AX = mybir.AxisListType.X
F32 = mybir.dt.float32
F32R = mybir.dt.float32r
BF16 = mybir.dt.bfloat16

P = 128
B, S, D = 4, 512, 256
T = B * S // P
QT = S // P
H, DH = 16, 16
C = D // P
FF = 1024
FC = FF // P
E = 4
HG = 4
G = B * H // HG
GB = H // HG
RING = 2
VW = DH + 2
TERMS = ((0, 0), (0, 1), (1, 0), (1, 1), (0, 2), (2, 0))
KS = len(TERMS) * DH
ROW_MAX = KS
LOWEST = -3.0e38
TIME_RATE = np.float32(-0.1)


def bf16_planes(a, n):
    out, rest = [], a.astype(np.float32)
    for _ in range(n):
        hi = (rest.view(np.uint32) & np.uint32(0xFFFF0000)).view(np.float32)
        out.append(hi)
        rest = (rest - hi).astype(np.float32)
    return out


def constants():
    t = np.arange(S)
    rate_t = (np.float32(0.1) * (t - S // 2).astype(np.float32)).astype(np.float32)
    tile = t // P
    sign = np.where(tile[None, :] >= np.arange(QT)[:, None], 1.0, -1.0).astype(np.float32)
    here = (tile[None, :] == np.arange(QT)[:, None]).astype(np.float32)
    q_rows, k_rows = [np.zeros(S, np.float32)], [np.ones(S, np.float32)]
    planes = bf16_planes(rate_t, 3)
    for k in range(QT):
        for p in planes:
            q_rows.append(-p * sign[k])
            k_rows.append(here[k])
            q_rows.append(sign[k])
            k_rows.append(here[k] * p)
    p = np.arange(P)
    behind = 2.0 * np.maximum(p[:, None] - p[None, :], 0)
    bias = TIME_RATE * np.abs(t[:, None] - t[None, :]).astype(np.float32)
    bias = bias.reshape(QT, P, S).transpose(1, 0, 2)
    return {
        "rows_q": np.stack(q_rows).astype(np.float32),
        "rows_k": np.stack(k_rows).astype(np.float32),
        "behind": behind.astype(np.float32),
        "time_bias": np.ascontiguousarray(bias, dtype=np.float32),
        "ident": np.eye(P, dtype=np.float32),
        "order": np.broadcast_to(np.arange(E, 0, -1, dtype=np.float32), (P, E)).copy(),
    }


NR = 1 + 6 * QT


def gated_blocks_program(nc, a, out):
    with ExitStack() as ctx:
        def dram(name, shape, dt):
            return nc.dram_tensor(name, shape, dt, kind="Internal").ap()

        def sb(name, shape, dt=F32, scope=ctx):
            return scope.enter_context(nc.sbuf_tensor(name, shape, dt))

        planes_dram = {(l, s): dram(f"planes_{l}_{s}", [3, D, B * S], BF16) for l in range(2) for s in "qk"}

        x = sb("x", [P, T, D])
        xT = sb("xT", [P, C, B * S])
        ctxT = sb("ctxT", [P, C, B * S])
        xn = sb("xn", [P, T, D])
        vals = sb("vals", [P, QT, B * H, VW])
        ident = sb("ident_sb", [P, P])
        w_qkv = {(l, s): sb(f"w_{l}_{s}", [P, C, D]) for l in range(2) for s in "qkv"}
        w_o = sb("w_o", [P, C, D])
        bias_v = sb("bias_v", [P, D])
        bias_o = sb("bias_o", [P, D])
        bias_2 = sb("bias_2", [P, D])
        bias_mo = sb("bias_mo", [P, D])
        gamma = sb("gamma", [P, D])
        beta = sb("beta", [P, D])
        bias_qk = sb("bias_qk", [P, 3, C])
        b1_cols = sb("b1_cols", [P, FC])
        gates_raw = sb("gates_raw", [P, 4])
        gates = sb("gates", [P, 4])
        stats = sb("stats", [P, T, 6])
        meanvar = sb("meanvar", [P, T, 2])
        rstd = sb("rstd", [P, T])
        var_eps = sb("var_eps", [P, T])
        root = sb("root", [P, T])
        newton = sb("newton", [P, T])
        minus_half = sb("minus_half", [P, T])
        tmp = sb("tmp", [P, 2, D])
        order = sb("order_sb", [P, E])
        w_router = sb("w_router", [P, C, E])
        ones = sb("ones", [P, P])
        quant = sb("quant", [P, 8])
        logits = sb("logits", [P, T, E])
        top = sb("top", [P, T])
        onehot = sb("onehot", [P, T, E])

        with ExitStack() as att:
            stack_q = sb("stack_q", [P, RING * H * S], BF16, att)
            stack_k = sb("stack_k", [P, RING * H * S], BF16, att)
            time_bias = sb("time_bias_sb", [P, QT, S], F32, att)
            biased = sb("biased", [P, 2, S], BF16, att)
            behind_raw = sb("behind_raw", [P, P], F32, att)
            behind = sb("behind_sb", [P, P], F32R, att)
            rate_eye = sb("rate_eye", [P, 2, P], F32R, att)
            rate_rest = sb("rate_rest", [P, P], F32, att)
            row_max = sb("row_max", [P, HG * QT], F32, att)
            row_max_t = sb("row_max_t", [P, P], BF16, att)
            recip = sb("recip", [P, HG * QT], F32, att)
            with ExitStack() as s1:
                full = sb("full", [P, 2, S], F32, s1)
                rest = sb("rest", [P, 2, S], F32, s1)
                planes = sb("planes", [P, 2, 3, S], BF16, s1)
            with ExitStack() as s1:
                probs = [sb(f"probs{i}", [P, QT * S], F32, s1) for i in range(2)]
        with ExitStack() as ffn:
            w1_raw = sb("w1_raw", [P, C, FF], F32, ffn)
            w2_raw = sb("w2_raw", [P, FC, D], F32, ffn)
            w1_q = sb("w1_q", [P, C, FF], F32, ffn)
            w2_q = sb("w2_q", [P, FC, D], F32, ffn)
            hid0 = sb("hid0", [P, 2, FC, S], F32, ffn)
        with ExitStack() as moe:
            w1_e = sb("w1_e", [P, E, C, FF], F32, moe)
            w_mo = sb("w_mo", [P, FC, D], F32, moe)
            b1_e = sb("b1_e", [P, FF], F32, moe)
            masked = sb("masked", [P, E * C, S], F32, moe)
            masked_nat = sb("masked_nat", [P, 2, E, D], F32, moe)
            onehotT = sb("onehotT", [P, S], F32, moe)
            hid1 = sb("hid1", [P, FC, S], F32, moe)
            y = sb("y", [P, 2, D], F32, moe)

        ps = [ctx.enter_context(nc.psum_tensor(f"ps_a{i}", [P, S], F32)) for i in range(2)]
        pw = [ctx.enter_context(nc.psum_tensor(f"ps_wide{i}", [P, 2 * S], F32)) for i in range(2)]
        po = ctx.enter_context(nc.psum_tensor("ps_out", [P, S], F32))
        pm = ctx.enter_context(nc.psum_tensor("ps_misc", [P, S], F32))

        def wide(k):
            return pw[(k // 2) % 2][:, (k % 2) * S:(k % 2) * S + S]

        sems = {}

        def sem(name):
            if name not in sems:
                sems[name] = ctx.enter_context(nc.semaphore(name))
            return sems[name]

        def wait(eng, s, v):
            if not isinstance(v, int) or v > 0:
                eng.wait_ge(s, v)

        loaded_first, loaded_rest, loaded_att = sem("loaded_first"), sem("loaded_rest"), sem("loaded_att")
        N_FIRST, N_REST, N_ATT = 9, 11, 4
        block = ctx.enter_context(nc.Block())

        def part(v):
            return v.rearrange("(c p) n -> p c n", p=P)

        def slot(g, j=0):
            return ((g & (RING * GB - 1)) * HG + j) * S

        @block.sync
        def _(sp):
            for dst, src in (
                (w_qkv[0, "k"][:], part(a["L0_Wk"])), (ctxT[:], part(a["ctxT"])), (w_qkv[0, "v"][:], part(a["L0_Wv"])),
                (bias_qk[:, 0, :], a["L0_bq"]), (bias_qk[:, 1, :], a["L0_bk"]),
                (bias_v[:], a["L0_bv"].partition_broadcast(P)), (ident[:], a["ident"]),
                (x[:], a["x"].rearrange("(t p) d -> p t d", p=P)), (w_qkv[0, "q"][:], part(a["L0_Wq"])),
            ):
                sp.dma_start(dst, src).then_inc(loaded_first, 16)
            for dst, src in (
                (w_o[:], part(a["L0_Wo"])), (gates_raw[:], a["gates"].partition_broadcast(P)),
                (bias_o[:], a["L0_bo"].partition_broadcast(P)), (bias_2[:], a["L0_b2"].partition_broadcast(P)),
                (b1_cols[:], a["L0_b1"]), (w_qkv[1, "q"][:], part(a["L1_Wq"])), (w_qkv[1, "k"][:], part(a["L1_Wk"])),
                (w_qkv[1, "v"][:], part(a["L1_Wv"])), (time_bias[:], a["time_bias"]),
                (behind_raw[:], a["behind"]), (order[:], a["order"]),
            ):
                sp.dma_start(dst, src).then_inc(loaded_rest, 16)
            for s_, rows in ((stack_q, a["rows_q"]), (stack_k, a["rows_k"])):
                for half in range(2):
                    dst = s_[KS:KS + NR, :].rearrange("r (h t) -> r h t", t=S)[:, half * H:(half + 1) * H]
                    sp.dma_start(dst, rows.unsqueeze(1).broadcast_to([NR, H, S])).then_inc(loaded_att, 16)
            for l in range(2):
                planes_ready, planes_kept = sem(f"planes_ready{l}"), [sem(f"planes_kept{l}_{i}") for i in range(2)]
                stacks_loaded, s2_done = sem(f"stacks_loaded{l}"), sem(f"scores_done{l}")
                u = 0
                for s_ in "kq":
                    for b in range(B):
                        for c in range(C):
                            sp.wait_ge(planes_ready, u + 1)
                            dst = planes_dram[l, s_][:, c * P:(c + 1) * P, b * S:(b + 1) * S]
                            sp.dma_start(dst.rearrange("n p t -> p n t"), planes[:, u % 2]).then_inc(planes_kept[u % 2], 16)
                            u += 1
                if l == 1:
                    sp.wait_ge(sem("down0_done"), T)
                    ones_row = a["rows_k"][0:1].unsqueeze(1).broadcast_to([1, RING * H, S])
                    sp.dma_start(stack_k[KS:KS + 1, :].rearrange("r (h t) -> r h t", t=S), ones_row
                                 ).then_inc(sem("ones_back"), 16)
                n = 0
                for b in range(B):
                    if b == 0:
                        for kept in planes_kept:
                            sp.wait_ge(kept, 16 * (u // 2))
                    else:
                        sp.wait_ge(stacks_loaded, 16 * n)
                    if b >= RING:
                        sp.wait_ge(s2_done, 2 * H * (b - RING + 1))
                    for i, terms in enumerate(TERMS):
                        for s_, stack, pl in (("q", stack_q, terms[0]), ("k", stack_k, terms[1])):
                            src = planes_dram[l, s_][pl, :, b * S:(b + 1) * S].rearrange("(h d) t -> d h t", d=DH)
                            dst = stack[i * DH:(i + 1) * DH, (b % RING) * H * S:(b % RING + 1) * H * S]
                            sp.dma_start(dst.rearrange("d (h t) -> d h t", t=S), src).then_inc(stacks_loaded, 16)
                            n += 1
                if l == 0:
                    sp.wait_ge(sem("pv_done0"), B * H)
                    sp.dma_start(w1_raw[:], part(a["L0_W1"])).then_inc(sem("w_ffn0"), 16)
                    sp.dma_start(w2_raw[:], part(a["L0_W2"])).then_inc(sem("w_ffn0"), 16)
            sp.wait_ge(sem("pv_done1"), B * H)
            sp.dma_start(w1_e[:], a["L1_W1"].rearrange("e (c p) n -> p e c n", p=P)).then_inc(sem("w_ffn1"), 16)
            for dst, src in ((w_mo[:], part(a["L1_Wo"])), (b1_e[0:E, :], a["L1_b1"]), (w_router[:], part(a["L1_Wr"])),
                             (bias_mo[:], a["L1_bo"].partition_broadcast(P)),
                             (gamma[:], a["gamma"].partition_broadcast(P)), (beta[:], a["beta"].partition_broadcast(P))):
                sp.dma_start(dst, src).then_inc(sem("w_ffn1"), 16)
            for t in range(T):
                sp.wait_ge(sem("x_final"), t + 1)
                sp.dma_start(out[t * P:(t + 1) * P, :], x[:, t, :]).then_inc(sem("stored"), 16)
            sp.wait_ge(sem("stored"), 16 * T)

        @block.tensor
        def _(pe):
            mm, tr = nc.tensor.matmul, nc.tensor.transpose

            def project(l, s_, u0, src, src_ready):
                for b in range(B):
                    src_ready(b)
                    for c in range(C):
                        u = u0 + b * C + c
                        wait(pe, sem(f"proj_read{l}"), u - 1)
                        for k in range(C):
                            last = mm(ps[u % 2][:], w_qkv[l, s_][:, k, c * P:(c + 1) * P],
                                      src[:, k, b * S:(b + 1) * S], start=(k == 0), stop=(k == C - 1))
                        last.then_inc(sem(f"proj_done{l}"), 1)

            def values(l):
                for v in range(T // 2):
                    wait(pe, sem(f"vals_read{l}"), v - 3)
                    for i in range(2):
                        t = 2 * v + i
                        for k in range(C):
                            last = mm(wide(v)[:, i * D:(i + 1) * D], ctxT[:, k, t * P:(t + 1) * P], w_qkv[l, "v"][:, k, :],
                                      start=(k == 0), stop=(k == C - 1))
                    last.then_inc(sem(f"vals_done{l}"), 1)

            def turn(name, src, before):
                done, read = sem(f"turned_{name}"), sem(f"turned_read_{name}")
                for b in range(B):
                    for c in range(C):
                        u = b * C + c
                        before(b, u)
                        wait(pe, read, u - 3)
                        for i in range(QT):
                            last = tr(wide(u)[:, i * P:(i + 1) * P], src(b * QT + i, c), ident[:])
                        last.then_inc(done, 1)

            def attention(l):
                s1_done, max_done = sem(f"s1_done{l}"), sem(f"max_done{l}")
                s2_done, exp_done = sem(f"scores_done{l}"), sem(f"exp_done{l}")
                pv_done, o_read = sem(f"pv_done{l}"), sem(f"o_read{l}")
                turned, sent = sem(f"max_turned{l}"), sem(f"max_sent{l}")
                rows = KS + (NR if l == 0 else 1)

                def for_maximum(g, j):
                    for q in range(QT):
                        wait(pe, max_done, (g * HG + j) * QT + q - 1)
                        mm(ps[q % 2][:], stack_q[0:KS, bass.ds(slot(g, j) + q * P, P)],
                           stack_k[0:KS, bass.ds(slot(g, j), S)], start=True, stop=True).then_inc(s1_done, 1)

                def turn_maximum(g):
                    wait(pe, max_done, (g + 1) * HG * QT)
                    wait(pe, sem(f"max_copied{l}"), g)
                    tr(pm[0:HG * QT, 0:P], row_max[:], ident[:]).then_inc(turned, 1)

                def scores(g, j):
                    if j == 0:
                        pe.wait_ge(sent, 16 * (g + 1))
                    for half in range(2):
                        wait(pe, exp_done, (g * HG + j) * 2 + half - 1)
                        for i in range(2):
                            k = 2 * half + i
                            last = mm(pw[half][:, i * S:(i + 1) * S], stack_k[0:rows, bass.ds(slot(g, j) + k * P, P)],
                                      stack_q[0:rows, bass.ds(slot(g, j), S)], start=True, stop=(l == 1),
                                      skip_group_check=True)
                            if l == 0:
                                for p in range(2):
                                    last = mm(pw[half][:, i * S + k * P:i * S + (k + 1) * P], rate_eye[:, p, :], behind[:],
                                              start=False, stop=(p == 1), skip_group_check=True)
                        last.then_inc(s2_done, 1)

                def weigh(g, j):
                    pe.wait_ge(exp_done, (g * HG + j) * 2 + 2)
                    if j == 0:
                        wait(pe, o_read, g)
                    for q in range(QT):
                        for k in range(QT):
                            last = mm(po[:, (j * QT + q) * VW:(j * QT + q + 1) * VW],
                                      probs[j % 2][:, k * S + q * P:k * S + (q + 1) * P],
                                      vals[:, k, bass.ds(g * HG + j, 1), :], start=(k == 0), stop=(k == QT - 1))
                    last.then_inc(pv_done, 1)

                def group(g, first=False, ahead=True):
                    for j in range(HG):
                        scores(g, j)
                        if ahead:
                            for_maximum(g + 2, j)
                        if j == 0 and not first:
                            weigh(g - 1, HG - 1)
                        if j > 0:
                            weigh(g, j - 1)
                    if ahead:
                        turn_maximum(g + 2)

                if l == 0:
                    pe.wait_ge(loaded_att, 16 * N_ATT)
                else:
                    pe.wait_ge(sem("ones_back"), 16)
                pe.wait_ge(sem(f"stacks_loaded{l}"), 16 * 12)
                for g in range(2):
                    for j in range(HG):
                        for_maximum(g, j)
                    turn_maximum(g)
                pe.wait_ge(sem(f"vals_read{l}"), T // 2)
                group(0, first=True)
                group(1)
                pe.wait_ge(sem(f"stacks_loaded{l}"), 16 * 24)
                with pe.Fori(2, G - 2) as g:
                    pe.wait_ge(sem(f"stacks_loaded{l}"), ((g + 2) >> 2) * (16 * 12) + 16 * 12)
                    group(g)
                group(G - 2, ahead=False)
                group(G - 1, ahead=False)
                weigh(G - 1, HG - 1)

            pe.wait_ge(loaded_first, 16 * N_FIRST)
            for l in range(2):
                n = 2 * l
                project(l, "k", 0, ctxT, lambda b: None)
                if l == 1:
                    pe.wait_ge(sem("proj_read1"), 1)
                values(l)
                turn(f"n{n}", lambda t, c: xn[:, t, c * P:(c + 1) * P], lambda b, u, l=l, n=n: (
                    wait(pe, sem(f"vals_read{l}"), min(u + 5, 8)), wait(pe, sem(f"normed{n}"), QT * (b + 1))))
                project(l, "q", B * C, xT, lambda b, n=n: wait(pe, sem(f"turned_read_n{n}"), C * (b + 1)))
                if l == 0:
                    pe.wait_ge(sem("rate_ready"), 3)
                pe.wait_ge(sem(f"proj_read{l}"), 2 * B * C)
                attention(l)
                if l == 0:
                    turn("att", lambda t, c: xn[:, t, c * P:(c + 1) * P], lambda b, u: (wait(pe, sem("exp_done0"), 2 * B * H),
                                                        wait(pe, sem("o_read0"), (b + 1) * GB)))
                    for t in range(T):
                        wait(pe, sem("turned_read_att"), C * (t // QT + 1))
                        wait(pe, sem("oproj_read"), t - 1)
                        for k in range(C):
                            last = mm(ps[t % 2][:, 0:D], xT[:, k, t * P:(t + 1) * P], w_o[:, k, :],
                                      start=(k == 0), stop=(k == C - 1))
                        last.then_inc(sem("oproj_done"), 1)
                    for w in range(2):
                        pe.wait_ge(sem("abs_sum"), w + 1)
                        if w == 0:
                            pe.wait_ge(sem("max_copied0"), G)
                        mm(pm[:, w:w + 1], ones[:], quant[:, w:w + 1], start=True, stop=True).then_inc(sem("gamma_done"), 1)
                    turn("n1", lambda t, c: xn[:, t, c * P:(c + 1) * P],
                         lambda b, u: (wait(pe, sem("turned_read_att"), B * C), wait(pe, sem("normed1"), QT * (b + 1))))
                    pe.wait_ge(sem("w_quant"), 4)
                    pe.wait_ge(sem("oproj_read"), T)
                    for b in range(B + 1):
                        if b < B:
                            pe.wait_ge(sem("turned_read_n1"), C * (b + 1))
                            for f in range(FC):
                                u = b * FC + f
                                wait(pe, sem("hid0_done"), u - 1)
                                for k in range(C):
                                    last = mm(ps[u % 2][:], w1_q[:, k, f * P:(f + 1) * P], xT[:, k, b * S:(b + 1) * S],
                                              start=(k == 0), stop=(k == C - 1))
                                last.then_inc(sem("up0_done"), 1)
                        if b > 0:
                            pe.wait_ge(sem("hid0_done"), b * FC)
                            for q in range(QT):
                                t = (b - 1) * QT + q
                                wait(pe, sem("down0_read"), t - 1)
                                for f in range(FC):
                                    last = mm((po, pm)[t % 2][:, 0:D], hid0[:, (b - 1) % 2, f, q * P:(q + 1) * P], w2_q[:, f, :],
                                              start=(f == 0), stop=(f == FC - 1))
                                last.then_inc(sem("down0_done"), 1)
            pe.wait_ge(sem("w_ffn1"), 16 * 7)
            pe.wait_ge(sem("exp_done1"), 2 * B * H)
            turn("n3", lambda t, c: xn[:, t, c * P:(c + 1) * P], lambda b, u: wait(pe, sem("normed3"), QT * (b + 1)))
            pe.wait_ge(sem("max_copied1"), G)
            for t in range(T):
                pe.wait_ge(sem("turned_read_n3"), C * (t // QT + 1))
                for k in range(C):
                    last = mm(pm[:, t * E:(t + 1) * E], xT[:, k, t * P:(t + 1) * P], w_router[:, k, :],
                              start=(k == 0), stop=(k == C - 1))
            last.then_inc(sem("logits_done"), 1)
            for b in range(B):
                for q in range(QT):
                    t = b * QT + q
                    pe.wait_ge(sem("masked_done"), t + 1)
                    for e2 in range(2):
                        u = 2 * t + e2
                        wait(pe, sem("masked_read"), u - 3)
                        if u < 4:
                            pe.wait_ge(sem("turned_read_n3"), B * C)
                        for i in range(4):
                            last = tr(wide(u)[:, i * P:(i + 1) * P],
                                      masked_nat[:, t % 2, 2 * e2 + i // C, (i % C) * P:(i % C + 1) * P], ident[:])
                        last.then_inc(sem("masked_turned"), 1)
                if b == 0:
                    pe.wait_ge(sem("routed"), 1)
                    pe.wait_ge(sem("logits_read"), 1)
                wait(pe, sem("hot_read"), b)
                wait(pe, sem("down1_read"), QT * b)
                for q in range(QT):
                    last = tr(pm[0:E, q * P:(q + 1) * P], onehot[:, b * QT + q, :], ident[:])
                last.then_inc(sem("hot_turned"), 1)
                pe.wait_ge(sem("masked_read"), 2 * QT * (b + 1))
                pe.wait_ge(sem("hot_read"), b + 1)
                for f in range(FC):
                    u = b * FC + f
                    wait(pe, sem("hid1_done"), u - 1)
                    mm(ps[u % 2][:], b1_e[0:E, f * P:(f + 1) * P], onehotT[0:E, :], start=True, stop=False)
                    for k in range(E * C):
                        last = mm(ps[u % 2][:], w1_e[:, k // C, k % C, f * P:(f + 1) * P], masked[:, k, :],
                                  start=False, stop=(k == E * C - 1))
                    last.then_inc(sem("up1_done"), 1)
                pe.wait_ge(sem("hid1_done"), (b + 1) * FC)
                for q in range(QT):
                    t = b * QT + q
                    wait(pe, sem("down1_read"), t - 1)
                    if t < 2:
                        pe.wait_ge(sem("hot_read"), 1)
                    for f in range(FC):
                        last = mm((po, pm)[t % 2][:, 0:D], hid1[:, f, q * P:(q + 1) * P], w_mo[:, f, :],
                                  start=(f == 0), stop=(f == FC - 1))
                    last.then_inc(sem("down1_done"), 1)

        @block.scalar
        def _(act):
            do = nc.scalar.activation

            def project_out(l, s_, u0):
                done, read, fulls = sem(f"proj_done{l}"), sem(f"proj_read{l}"), sem(f"full{l}")
                n = B * C
                for i in range(n + 1):
                    u = u0 + i
                    if i < n:
                        act.wait_ge(done, u + 1)
                        wait(act, sem(f"planes_ready{l}"), u - 1)
                        if l == 0:
                            c = u % C
                            ins = do(full[:, u % 2, :], ps[u % 2][:], ACT.Identity,
                                     bias=bias_qk[:, 2 if s_ == "q" else 1, c:c + 1], scale=0.25 if s_ == "q" else 1.0)
                        else:
                            ins = do(full[:, u % 2, :], ps[u % 2][:], ACT.Relu, scale=0.25 if s_ == "q" else 1.0)
                        ins.then_inc(read, 1)
                    if i > 0:
                        act.wait_ge(sem(f"rest{l}"), u)
                        do(planes[:, (u - 1) % 2, 1, :], rest[:, (u - 1) % 2, :], ACT.Copy).then_inc(sem(f"middle{l}"), 1)

            def turned_out(name, order_of=lambda b, c: None):
                for b in range(B):
                    for c in range(C):
                        u = b * C + c
                        act.wait_ge(sem(f"turned_{name}"), u + 1)
                        do(xT[:, c, b * S:(b + 1) * S], wide(u), ACT.Copy).then_inc(sem(f"turned_read_{name}"), 1)

            def attention(l):
                s2_done, exp_done, pv_done = sem(f"scores_done{l}"), sem(f"exp_done{l}"), sem(f"pv_done{l}")
                turned, copied, sent = sem(f"max_turned{l}"), sem(f"max_copied{l}"), sem(f"max_sent{l}")

                def send_maximum(g):
                    act.wait_ge(turned, g + 1)
                    wait(act, sent, 16 * g)
                    do(row_max_t[0:HG * QT, :], pm[0:HG * QT, 0:P], ACT.Copy, scale=-1.0).then_inc(copied, 1)
                    act.wait_ge(copied, g + 1)
                    act.dma_start(stack_q[ROW_MAX:ROW_MAX + 1, bass.ds(slot(g), HG * S)],
                                  row_max_t[0:HG * QT, :]).then_inc(sent, 16)

                def group(g, ahead=True):
                    for j in range(HG):
                        for half in range(2):
                            n = (g * HG + j) * 2 + half
                            act.wait_ge(s2_done, n + 1)
                            if half == 0:
                                wait(act, pv_done, g * HG + j - 1)
                            do(probs[j % 2][:, half * 2 * S:(half + 1) * 2 * S], pw[half][:], ACT.Exp).then_inc(exp_done, 1)
                    if ahead:
                        send_maximum(g + 2)

                send_maximum(0)
                send_maximum(1)
                for i in range(2):
                    act.wait_ge(sem(f"planes_kept{l}_{i}"), 16 * B * C)
                group(0)
                with act.Fori(1, G - 2) as g:
                    group(g)
                group(G - 2, ahead=False)
                group(G - 1, ahead=False)

            act.wait_ge(loaded_first, 16 * N_FIRST)
            act.wait_ge(loaded_rest, 16 * N_REST)
            act.wait_ge(sem("prepared"), 1)
            do(gates[:], gates_raw[:], ACT.Tanh).then_inc(sem("gates"), 1)
            for l in range(2):
                if l == 1:
                    act.wait_ge(sem("down0_done"), T)
                project_out(l, "k", 0)
                turned_out(f"n{2 * l}")
                project_out(l, "q", B * C)
                attention(l)
                if l == 0:
                    turned_out("att")
                    act.wait_ge(sem("w_ffn0"), 32)
                    for w, raw in enumerate((w1_raw, w2_raw)):
                        do(hid0[:, w].rearrange("p f s -> p (f s)")[:, 0:C * FF], raw[:].rearrange("p c n -> p (c n)"),
                           ACT.Abs, accum_out=quant[:, w:w + 1]).then_inc(sem("abs_sum"), 1)
                    turned_out("n1")
                    act.wait_ge(sem("abs_sum"), 2)
                    for b in range(B):
                        wait(act, sem("down0_done"), QT * (b - 1))
                        for f in range(FC):
                            u = b * FC + f
                            act.wait_ge(sem("up0_done"), u + 1)
                            do(hid0[:, b % 2, f, :], ps[u % 2][:], ACT.Relu, bias=b1_cols[:, f:f + 1]
                               ).then_inc(sem("hid0_done"), 1)
            turned_out("n3")
            for b in range(B):
                wait(act, sem("down1_done"), QT * b)
                for f in range(FC):
                    u = b * FC + f
                    act.wait_ge(sem("up1_done"), u + 1)
                    do(hid1[:, f, :], ps[u % 2][:], ACT.Gelu).then_inc(sem("hid1_done"), 1)

        @block.gpsimd
        def _(pool):
            nc.gpsimd.memset(minus_half[:], -0.5).then_inc(sem("half_ready"), 1)
            pool.wait_ge(sem("half_ready"), 1)
            for i in range(4 + T):
                t0, t1 = (0, T) if i < 4 else (i - 4, i - 3)
                pool.wait_ge(sem("var_ready"), i + 1)
                nc.gpsimd.tensor_tensor(root[:, t0:t1], var_eps[:, t0:t1], minus_half[:, t0:t1], ALU.pow
                                        ).then_inc(sem("root_ready"), 1)

        @block.vector
        def _(dve):
            v = nc.vector

            rooted = [0]

            def inverse_root(n, t0, t1, eps):
                w, r, h, y1 = (z[:, t0:t1] for z in (var_eps, root, newton, rstd))
                rooted[0] += 1
                st, k = sem("newton_step"), 4 * rooted[0] - 4
                v.tensor_scalar(w, meanvar[:, t0:t1, 1], eps, None, ALU.add).then_inc(sem("var_ready"), 1)
                dve.wait_ge(sem("root_ready"), rooted[0])
                v.tensor_tensor(h, r, r, ALU.mult).then_inc(st, 1)
                dve.wait_ge(st, k + 1)
                v.tensor_tensor(h, h, w, ALU.mult).then_inc(st, 1)
                dve.wait_ge(st, k + 2)
                v.tensor_scalar(h, h, -0.5, 1.5, ALU.mult, ALU.add).then_inc(st, 1)
                dve.wait_ge(st, k + 3)
                v.tensor_tensor(y1, h, r, ALU.mult).then_inc(st, 1)
                dve.wait_ge(st, k + 4)

            def norm_stats(n, eps):
                s_, ag = sem(f"stats{n}"), sem(f"aggr{n}")
                with dve.Fori(0, T) as t:
                    v.bn_stats(stats[:, bass.ds(t, 1), :], x[:, bass.ds(t, 1), :]).then_inc(s_, 1)
                dve.wait_ge(s_, T)
                for t in range(T):
                    v.bn_aggr(meanvar[:, t, :], stats[:, t, :]).then_inc(ag, 1)
                dve.wait_ge(ag, T)
                inverse_root(n, 0, T, eps)

            def norm(n):
                norm_stats(n, 1e-5)
                for t in range(T):
                    v.tensor_scalar(xn[:, t, :], x[:, t, :], meanvar[:, t, 0:1], rstd[:, t:t + 1],
                                    ALU.subtract, ALU.mult).then_inc(sem(f"normed{n}"), 1)

            def split(l, u0):
                hi, rs = sem(f"high{l}"), sem(f"rest{l}")
                n = B * C
                for i in range(n + 1):
                    u = u0 + i
                    if i < n:
                        dve.wait_ge(sem(f"proj_read{l}"), u + 1)
                        wait(dve, sem(f"planes_kept{l}_{u % 2}"), 16 * (u // 2))
                        v.tensor_copy(planes[:, u % 2, 0, :], full[:, u % 2, :]).then_inc(hi, 1)
                        dve.wait_ge(hi, u + 1)
                        v.tensor_tensor(rest[:, u % 2, :], full[:, u % 2, :], planes[:, u % 2, 0, :],
                                        ALU.subtract).then_inc(rs, 1)
                    if i > 0:
                        dve.wait_ge(sem(f"middle{l}"), u)
                        v.tensor_tensor(planes[:, (u - 1) % 2, 2, :], rest[:, (u - 1) % 2, :], planes[:, (u - 1) % 2, 1, :],
                                        ALU.subtract).then_inc(sem(f"planes_ready{l}"), 1)

            def values(l):
                for k in range(T // 2):
                    dve.wait_ge(sem(f"vals_done{l}"), k + 1)
                    for i in range(2):
                        b, q = divmod(2 * k + i, QT)
                        dst = vals[:, q, b * H:(b + 1) * H, 0:DH]
                        src = wide(k)[:, i * D:(i + 1) * D].rearrange("p (h d) -> p h d", d=DH)
                        if l == 0:
                            ins = v.tensor_tensor(dst, src, bias_v[:].rearrange("p (h d) -> p h d", d=DH), ALU.add)
                        else:
                            ins = v.tensor_scalar(dst, src, 0.0, None, ALU.max)
                    ins.then_inc(sem(f"vals_read{l}"), 1)

            def attention(l):
                s1_done, max_done = sem(f"s1_done{l}"), sem(f"max_done{l}")
                pv_done, o_read, turned = sem(f"pv_done{l}"), sem(f"o_read{l}"), sem(f"max_turned{l}")

                def maxima(g, j):
                    if j == 0:
                        wait(dve, turned, g)
                    for q in range(QT):
                        dst = row_max[:, j * QT + q:j * QT + q + 1]
                        dve.wait_ge(s1_done, (g * HG + j) * QT + q + 1)
                        if l == 0:
                            dve.sem_inc(sem("max_begun"), 1)
                            v.tensor_tensor_reduce(biased[:, q % 2, :], ps[q % 2][:], time_bias[:, q, :], 1.0, LOWEST,
                                                   ALU.add, ALU.max, dst).then_inc(max_done, 1)
                        else:
                            v.tensor_reduce(dst, ps[q % 2][:], AX, ALU.max).then_inc(max_done, 1)

                def normalise(g):
                    dve.wait_ge(pv_done, (g + 1) * HG)
                    o = po[:, 0:HG * QT * VW].rearrange("p (n w) -> p n w", w=VW)
                    v.reciprocal(recip[:], o[:, :, DH]).then_inc(sem(f"recip{l}"), 1)
                    dve.wait_ge(sem(f"recip{l}"), g + 1)
                    by_group = xn[:].rearrange("p (b q) (n j d) -> p b n q j d", q=QT, n=GB, d=DH)
                    dst = by_group[:, bass.ds(g >> 2, 1), bass.ds(g & 3, 1)].rearrange("p b n q j d -> p (b n q) j d")
                    v.tensor_tensor(dst, o[:, :, 0:DH].rearrange("p (j q) d -> p q j d", q=QT),
                                    recip[:].rearrange("p (j q) -> p q j", q=QT).unsqueeze(3).broadcast_to([P, QT, HG, DH]),
                                    ALU.mult).then_inc(o_read, 1)

                def group(g, first=False, ahead=True):
                    for j in range(HG):
                        if ahead:
                            maxima(g + 2, j)
                        if j == 0 and not first:
                            normalise(g - 1)

                for g in range(2):
                    for j in range(HG):
                        maxima(g, j)
                group(0, first=True)
                with dve.Fori(1, G - 2) as g:
                    group(g)
                group(G - 2, ahead=False)
                group(G - 1, ahead=False)
                normalise(G - 1)

            def quantise():
                dve.wait_ge(sem("gamma_done"), 2)
                v.tensor_scalar(quant[:, 2:4], pm[:, 0:2], 1.0 / (D * FF), 1e-5, ALU.mult, ALU.add).then_inc(sem("q_step"), 1)
                dve.wait_ge(sem("q_step"), 1)
                v.tensor_scalar(quant[:, 4:6], quant[:, 2:4], 0.5, None, ALU.mult).then_inc(sem("q_step"), 1)
                v.tensor_scalar(quant[:, 6:8], quant[:, 2:4], -0.5, None, ALU.mult).then_inc(sem("q_step"), 1)
                dve.wait_ge(sem("q_step"), 3)
                for w, (raw, q) in enumerate(((w1_raw, w1_q), (w2_raw, w2_q))):
                    v.tensor_scalar(q[:], raw[:], quant[:, 6 + w:7 + w], None, ALU.is_lt).then_inc(sem("w_quant"), 1)
                    dve.wait_ge(sem("w_quant"), 2 * w + 1)
                    v.scalar_tensor_tensor(out=q[:], in0=raw[:], scalar=quant[:, 4 + w:5 + w], in1=q[:],
                                           op0=ALU.is_gt, op1=ALU.subtract).then_inc(sem("w_quant"), 1)

            def add_gated(name, t, src, bias, gate):
                v.tensor_tensor(tmp[:, t % 2, :], src, bias, ALU.add).then_inc(sem(name), 1)
                dve.wait_ge(sem(name), t + 1)
                return v.scalar_tensor_tensor(out=x[:, t, :], in0=tmp[:, t % 2, :], scalar=gates[:, gate:gate + 1],
                                              in1=x[:, t, :], op0=ALU.mult, op1=ALU.add)

            v.memset(ones[:], 1.0).then_inc(sem("dve_const"), 1)
            v.memset(vals[:, :, :, DH:VW], 1.0).then_inc(sem("dve_const"), 1)
            dve.wait_ge(loaded_first, 16 * N_FIRST)
            v.tensor_scalar(bias_qk[:, 2, :], bias_qk[:, 0, :], 0.25, None, ALU.mult).then_inc(sem("prepared"), 1)
            norm(0)
            dve.wait_ge(loaded_rest, 16 * N_REST)
            v.tensor_copy(behind[:], behind_raw[:]).then_inc(sem("rate_ready"), 1)
            v.tensor_scalar(rate_eye[:, 0, :], ident[:], float(TIME_RATE), None, ALU.mult).then_inc(sem("rate_ready"), 1)
            dve.wait_ge(sem("rate_ready"), 2)
            v.scalar_tensor_tensor(out=rate_eye[:, 1, :], in0=ident[:], scalar=float(TIME_RATE), in1=rate_eye[:, 0, :],
                                   op0=ALU.mult, op1=ALU.subtract).then_inc(sem("rate_ready"), 1)
            dve.wait_ge(sem("rate_ready"), 3)

            for l in range(2):
                if l == 1:
                    norm(2)
                split(l, 0)
                values(l)
                split(l, B * C)
                attention(l)
                if l == 0:
                    dve.wait_ge(sem("gates"), 1)
                    for t in range(T):
                        dve.wait_ge(sem("oproj_done"), t + 1)
                        ins = add_gated("oproj_tmp", t, ps[t % 2][:, 0:D], bias_o[:], 0)
                        ins.then_inc(sem("oproj_read"), 1)
                    dve.wait_ge(sem("oproj_read"), T)
                    dve.wait_ge(sem("turned_att"), B * C)
                    norm(1)
                    dve.wait_ge(sem("w_ffn0"), 32)
                    quantise()
                    for t in range(T):
                        dve.wait_ge(sem("down0_done"), t + 1)
                        ins = add_gated("down0_tmp", t, (po, pm)[t % 2][:, 0:D], bias_2[:], 2)
                        ins.then_inc(sem("down0_read"), 1)
                    dve.wait_ge(sem("down0_read"), T)
            dve.wait_ge(sem("o_read1"), G)
            for t in range(T):
                v.scalar_tensor_tensor(out=x[:, t, :], in0=xn[:, t, :], scalar=gates[:, 1:2], in1=x[:, t, :],
                                       op0=ALU.mult, op1=ALU.add).then_inc(sem("x_att1"), 1)
            dve.wait_ge(sem("x_att1"), T)
            norm(3)
            dve.wait_ge(sem("logits_done"), 1)
            v.tensor_copy(logits[:], pm[:, 0:T * E].rearrange("p (t e) -> p t e", e=E)).then_inc(sem("logits_read"), 1)
            dve.wait_ge(sem("logits_read"), 1)
            rt = sem("route_step")
            v.tensor_reduce(top[:], logits[:], AX, ALU.max).then_inc(rt, 1)
            dve.wait_ge(rt, 1)
            v.tensor_tensor(onehot[:], logits[:], top[:].unsqueeze(2).broadcast_to([P, T, E]), ALU.is_equal).then_inc(rt, 1)
            dve.wait_ge(rt, 2)
            v.tensor_tensor(logits[:], onehot[:], order[:].unsqueeze(1).broadcast_to([P, T, E]), ALU.mult).then_inc(rt, 1)
            dve.wait_ge(rt, 3)
            v.tensor_reduce(top[:], logits[:], AX, ALU.max).then_inc(rt, 1)
            dve.wait_ge(rt, 4)
            v.tensor_tensor(onehot[:], logits[:], top[:].unsqueeze(2).broadcast_to([P, T, E]), ALU.is_equal).then_inc(sem("routed"), 1)
            dve.wait_ge(sem("routed"), 1)
            dve.wait_ge(sem("exp_done1"), 2 * B * H)
            dve.wait_ge(sem("w_ffn1"), 16 * 7)

            def mask(t):
                wait(dve, sem("masked_turned"), 2 * (t - 1))
                for e in range(E):
                    ins = v.tensor_scalar(masked_nat[:, t % 2, e, :], xn[:, t, :], onehot[:, t, e:e + 1], None, ALU.mult)
                ins.then_inc(sem("masked_done"), 1)

            for b in range(B):
                for q in range(QT + 1):
                    t = b * QT + q
                    if q < QT:
                        mask(t)
                    if q > 0:
                        wait(dve, sem("up1_done"), b * FC)
                        for e2 in range(2):
                            u = 2 * (t - 1) + e2
                            dve.wait_ge(sem("masked_turned"), u + 1)
                            v.tensor_copy(masked[:, 4 * e2:4 * e2 + 4, (q - 1) * P:q * P],
                                          wide(u).rearrange("p (n t) -> p n t", t=P)).then_inc(sem("masked_read"), 1)
                dve.wait_ge(sem("hot_turned"), b + 1)
                v.tensor_copy(onehotT[0:E, :], pm[0:E, :]).then_inc(sem("hot_read"), 1)
                for q in range(QT):
                    t = b * QT + q
                    dve.wait_ge(sem("down1_done"), t + 1)
                    st = sem("tail")
                    base = 7 * t
                    yt, k = y[:, t % 2, :], t % 2
                    v.tensor_tensor(yt, (po, pm)[t % 2][:, 0:D], bias_mo[:], ALU.add).then_inc(sem("down1_read"), 1)
                    dve.wait_ge(sem("down1_read"), t + 1)
                    v.tensor_tensor(yt, yt, xn[:, t, :], ALU.add).then_inc(st, 1)
                    dve.wait_ge(st, base + 1)
                    v.bn_stats(stats[:, t, :], yt).then_inc(st, 1)
                    dve.wait_ge(st, base + 2)
                    v.bn_aggr(meanvar[:, t, :], stats[:, t, :]).then_inc(st, 1)
                    dve.wait_ge(st, base + 3)
                    inverse_root(4, t, t + 1, 1e-12)
                    v.tensor_scalar(yt, yt, meanvar[:, t, 0:1], rstd[:, t:t + 1], ALU.subtract, ALU.mult).then_inc(st, 1)
                    dve.wait_ge(st, base + 4)
                    v.tensor_tensor(yt, yt, gamma[:], ALU.mult).then_inc(st, 1)
                    dve.wait_ge(st, base + 5)
                    v.tensor_tensor(yt, yt, beta[:], ALU.add).then_inc(st, 2)
                    dve.wait_ge(st, base + 7)
                    v.scalar_tensor_tensor(out=x[:, t, :], in0=yt, scalar=gates[:, 3:4], in1=x[:, t, :],
                                           op0=ALU.mult, op1=ALU.add).then_inc(sem("x_final"), 1)


def kernel(**inputs):
    import concourse.bacc as _bacc
    from concourse.bass_utils import run_bass_kernel_spmd as _run

    def host(name):
        return np.asarray(inputs[name])

    def cols(v):
        return v.reshape(-1, P).T

    lay = {
        "x": host("x").reshape(B * S, D), "ctxT": host("ctx_1024").reshape(B * S, D).T,
        "gates": np.concatenate([host("g_xattn"), host("g_ffn")]),
        "L0_Wq": host("L0_xattn_Wq").T, "L0_Wk": host("L0_xattn_Wk").T, "L0_Wv": host("L0_xattn_Wv").T,
        "L0_Wo": host("L0_xattn_Wo").T, "L0_bq": cols(host("L0_xattn_bq")), "L0_bk": cols(host("L0_xattn_bk")),
        "L0_bv": host("L0_xattn_bv"), "L0_bo": host("L0_xattn_bo"),
        "L0_W1": host("L0_ffn_W1").T, "L0_b1": cols(host("L0_ffn_b1")), "L0_W2": host("L0_ffn_W2").T,
        "L0_b2": host("L0_ffn_b2"),
        "L1_Wq": host("L1_xattn_Wq").T, "L1_Wk": host("L1_xattn_Wk").T, "L1_Wv": host("L1_xattn_Wv").T,
        "L1_Wr": host("L1_ffn_W_router"), "L1_W1": host("L1_ffn_W1"), "L1_b1": host("L1_ffn_b1"),
        "L1_Wo": host("L1_ffn_Wo"), "L1_bo": host("L1_ffn_bo"), "gamma": host("L1_ffn_ln_gamma"),
        "beta": host("L1_ffn_ln_beta"),
    }
    import ml_dtypes
    tables = constants()
    for name in ("rows_q", "rows_k"):
        tables[name] = tables[name].astype(ml_dtypes.bfloat16)
    lay.update(tables)
    nc = _bacc.Bacc("TRN2", target_bir_lowering=False, num_devices=1)
    arrays, args = {}, {}
    for name, v in lay.items():
        v = np.ascontiguousarray(v)
        arrays[f"in_{name}"] = v
        args[name] = nc.dram_tensor(f"in_{name}", v.shape, mybir.dt.from_np(v.dtype), kind="ExternalInput").ap()
    out = nc.dram_tensor("out_x", (B * S, D), F32, kind="ExternalOutput").ap()
    gated_blocks_program(nc, args, out)
    r = _run(nc, [arrays], core_ids=[0])
    return r.results[0]["out_x"].reshape(B, S, D)
```

```python
from contextlib import ExitStack

import numpy as np
import concourse.bass as bass
from concourse import mybir

ALU = mybir.AluOpType
ACT = mybir.ActivationFunctionType
AX = mybir.AxisListType.X
F32 = mybir.dt.float32
F32R = mybir.dt.float32r
BF16 = mybir.dt.bfloat16
F16 = mybir.dt.float16

P = 128
B, S, D = 4, 512, 256
T = B * S // P
QT = S // P
H, DH = 16, 16
C = D // P
FF = 1024
FC = FF // P
E = 4
HG = 4
G = B * H // HG
GB = H // HG
RING = 4
VP = 3
VW = VP * DH + 4
TERMS = ((0, 0), (1, 1), (0, 1), (0, 2), (1, 0), (2, 0))
RUNS_Q = ((0, 0, 2), (2, 0, 1), (3, 0, 1), (4, 1, 2))
RUNS_K = ((0, 0, 2), (2, 1, 2), (4, 0, 1), (5, 0, 1))
GIVES = len(RUNS_Q) + len(RUNS_K)
KS = len(TERMS) * DH
MP = 3
SCALE_LOG = 6.9375
LAG = 2
LOWEST = -3.0e38
LOW_DVE = (2, 6)
LOW_POOL = tuple(n for n in range(2 * HG) if n not in LOW_DVE)
TIME_RATE = np.float32(-0.1)


def bf16_planes(a, n):
    out, rest = [], a.astype(np.float32)
    for _ in range(n):
        hi = (rest.view(np.uint32) & np.uint32(0xFFFF0000)).view(np.float32)
        out.append(hi)
        rest = (rest - hi).astype(np.float32)
    return out


def constants():
    t = np.arange(S)
    rate_t = (np.float32(0.1) * (t - S // 2).astype(np.float32)).astype(np.float32)
    tile = t // P
    sign = np.where(tile[None, :] >= np.arange(QT)[:, None], 1.0, -1.0).astype(np.float32)
    here = (tile[None, :] == np.arange(QT)[:, None]).astype(np.float32)
    q_rows, k_rows = [np.zeros(S, np.float32)] * MP, [np.ones(S, np.float32)] * (MP + 1)
    q_rows.append(np.full(S, SCALE_LOG, np.float32))
    planes = bf16_planes(rate_t, 3)
    for k in range(QT):
        for p in planes:
            q_rows.append(-p * sign[k])
            k_rows.append(here[k])
            q_rows.append(sign[k])
            k_rows.append(here[k] * p)
    p = np.arange(P)
    behind = 2.0 * np.maximum(p[:, None] - p[None, :], 0)
    bias = TIME_RATE * np.abs(np.arange(2 * S - P)[None, :] - p[:, None] - (S - P)).astype(np.float32)
    return {
        "rows_q": np.stack(q_rows).astype(np.float32),
        "rows_k": np.stack(k_rows).astype(np.float32),
        "behind": behind.astype(np.float32),
        "time_bias": bias.astype(np.float32),
        "ident": np.eye(P, dtype=np.float32),
        "order": np.broadcast_to(np.arange(E, 0, -1, dtype=np.float32), (P, E)).copy(),
    }


NR = MP + 1 + 6 * QT


def gated_blocks_program(nc, a, out):
    with ExitStack() as ctx:
        def dram(name, shape, dt):
            return nc.dram_tensor(name, shape, dt, kind="Internal").ap()

        def sb(name, shape, dt=F32, scope=ctx):
            return scope.enter_context(nc.sbuf_tensor(name, shape, dt))

        planes_dram = {(l, s): dram(f"planes_{l}_{s}", [G, 3, DH, HG, S], BF16) for l in range(2) for s in "qk"}

        x = sb("x", [P, T, D])
        xT = sb("xT", [P, C, B * S])
        ctxT = sb("ctxT", [P, C, B * S])
        xn = sb("xn", [P, T, D])
        vals = sb("vals", [P, QT, B * H, VW], BF16)
        ident = sb("ident_sb", [P, P])
        w_qkv = {(l, s): sb(f"w_{l}_{s}", [P, C, D]) for l in range(2) for s in "qkv"}
        w_o = sb("w_o", [P, C, D])
        bias_v = sb("bias_v", [P, D])
        bias_o = sb("bias_o", [P, D])
        bias_2 = sb("bias_2", [P, D])
        bias_mo = sb("bias_mo", [P, D])
        gamma = sb("gamma", [P, D])
        beta = sb("beta", [P, D])
        bias_qk = sb("bias_qk", [P, 3, C])
        b1_cols = sb("b1_cols", [P, FC])
        gates_raw = sb("gates_raw", [P, 4])
        gates = sb("gates", [P, 4])
        stats = sb("stats", [P, T, 6])
        meanvar = sb("meanvar", [P, T, 2])
        rstd = sb("rstd", [P, T])
        var_eps = sb("var_eps", [P, T])
        root = sb("root", [P, T])
        newton = sb("newton", [P, T])
        minus_half = sb("minus_half", [P, T])
        tmp = sb("tmp", [P, 2, D])
        order = sb("order_sb", [P, E])
        w_router = sb("w_router", [P, C, E])
        ones = sb("ones", [P, P])
        quant = sb("quant", [P, 8])
        logits = sb("logits", [P, T, E])
        top = sb("top", [P, T])
        onehot = sb("onehot", [P, T, E])

        with ExitStack() as att:
            stack_q = sb("stack_q", [P, RING * HG * S], BF16, att)
            stack_k = sb("stack_k", [P, RING * HG * S], BF16, att)
            time_bias = sb("time_bias_sb", [P, 2 * S - P], F32, att)
            biased = sb("biased", [P, 2, S], BF16, att)
            behind_raw = sb("behind_raw", [P, P], F32, att)
            behind = sb("behind_sb", [P, P], F32R, att)
            rate_eye = sb("rate_eye", [P, 2, P], F32R, att)
            rate_rest = sb("rate_rest", [P, P], F32, att)
            row_max = sb("row_max", [P, HG * QT], F32, att)
            max_planes = sb("max_planes", [P, MP, P], BF16, att)
            max_rest = sb("max_rest", [P, P], F32, att)
            recip = sb("recip", [P, 2 * QT], F32, att)
            summed = sb("summed", [P, 2 * QT, DH], F32, att)
            with ExitStack() as s1:
                full = sb("full", [P, 2, S], F32, s1)
                rest = sb("rest", [P, 2, S], F32, s1)
                planes = sb("planes", [P, 2, 3, S], BF16, s1)
                v_full = sb("v_full", [P, 2, 2, D], F32, s1)
                v_rest = sb("v_rest", [P, 2, 2, D], F32, s1)
            with ExitStack() as s1:
                probs = [sb(f"probs{i}", [P, QT * S], F32, s1) for i in range(2)]
                probs_hi = [sb(f"probs_hi{i}", [P, QT * S], F16, s1) for i in range(HG)]
                probs_lo = [sb(f"probs_lo{i}", [P, QT * S], F16, s1) for i in range(HG)]
        with ExitStack() as ffn:
            w1_raw = sb("w1_raw", [P, C, FF], F32, ffn)
            w2_raw = sb("w2_raw", [P, FC, D], F32, ffn)
            w1_q = sb("w1_q", [P, C, FF], F32, ffn)
            w2_q = sb("w2_q", [P, FC, D], F32, ffn)
            hid0 = sb("hid0", [P, 2, FC, S], F32, ffn)
        with ExitStack() as moe:
            w1_e = sb("w1_e", [P, E, C, FF], F32, moe)
            w_mo = sb("w_mo", [P, FC, D], F32, moe)
            b1_e = sb("b1_e", [P, FF], F32, moe)
            masked = sb("masked", [P, E * C, S], F32, moe)
            masked_nat = sb("masked_nat", [P, 2, E, D], F32, moe)
            onehotT = sb("onehotT", [P, S], F32, moe)
            hid1 = sb("hid1", [P, FC, S], F32, moe)
            y = sb("y", [P, 2, D], F32, moe)

        ps = [ctx.enter_context(nc.psum_tensor(f"ps_a{i}", [P, S], F32)) for i in range(2)]
        pw = [ctx.enter_context(nc.psum_tensor(f"ps_wide{i}", [P, 2 * S], F32)) for i in range(2)]
        po = ctx.enter_context(nc.psum_tensor("ps_out", [P, S], F32))
        pm = ctx.enter_context(nc.psum_tensor("ps_misc", [P, S], F32))
        heads_out = (po, pm)

        def wide(k):
            return pw[(k // 2) % 2][:, (k % 2) * S:(k % 2) * S + S]

        sems = {}

        def sem(name):
            if name not in sems:
                sems[name] = ctx.enter_context(nc.semaphore(name))
            return sems[name]

        def wait(eng, s, v):
            if not isinstance(v, int) or v > 0:
                eng.wait_ge(s, v)

        def apart(eng, name):
            eng.sem_inc(sem(f"apart_{name}"), 1)

        loaded_first, loaded_rest, loaded_att = sem("loaded_first"), sem("loaded_rest"), sem("loaded_att")
        N_FIRST, N_REST, N_ATT = 9, 11, 2
        block = ctx.enter_context(nc.Block())

        def part(v):
            return v.rearrange("(c p) n -> p c n", p=P)

        def slot(g, j=0):
            return ((g & (RING - 1)) * HG + j) * S

        def vals_plane(i, p):
            b, q = divmod(2 * i, QT)
            return vals[:, q:q + 2, b * H:(b + 1) * H, p * DH:(p + 1) * DH]

        def halves(t, i):
            return t[:, i % 2].rearrange("p n (h d) -> p n h d", d=DH)

        def lows_done(eng, l, g, n):
            for name, own in (("pool", LOW_POOL), ("dve", LOW_DVE)):
                wait(eng, sem(f"low_{name}{l}"), g * len(own) + sum(m <= n for m in own) - sum(m > n + 2 * HG for m in own))

        def low_part(eng, ops, l, g, n):
            j, half = divmod(n, 2)
            eng.wait_ge(sem(f"exp_done{l}"), g * (2 * HG) + n + 1)
            cols = slice(half * 2 * S, (half + 1) * 2 * S)
            return ops.tensor_tensor(probs_lo[j][:, cols], probs[j % 2][:, cols], probs_hi[j][:, cols], ALU.subtract)

        @block.sync
        def _(sp):
            for dst, src in (
                (w_qkv[0, "k"][:], part(a["L0_Wk"])), (ctxT[:], part(a["ctxT"])), (w_qkv[0, "v"][:], part(a["L0_Wv"])),
                (bias_qk[:, 0, :], a["L0_bq"]), (bias_qk[:, 1, :], a["L0_bk"]),
                (bias_v[:], a["L0_bv"].partition_broadcast(P)), (ident[:], a["ident"]),
                (x[:], a["x"].rearrange("(t p) d -> p t d", p=P)), (w_qkv[0, "q"][:], part(a["L0_Wq"])),
            ):
                sp.dma_start(dst, src).then_inc(loaded_first, 16)
            for dst, src in (
                (w_o[:], part(a["L0_Wo"])), (gates_raw[:], a["gates"].partition_broadcast(P)),
                (bias_o[:], a["L0_bo"].partition_broadcast(P)), (bias_2[:], a["L0_b2"].partition_broadcast(P)),
                (b1_cols[:], a["L0_b1"]), (w_qkv[1, "q"][:], part(a["L1_Wq"])), (w_qkv[1, "k"][:], part(a["L1_Wk"])),
                (w_qkv[1, "v"][:], part(a["L1_Wv"])), (time_bias[:], a["time_bias"]),
                (behind_raw[:], a["behind"]), (order[:], a["order"]),
            ):
                sp.dma_start(dst, src).then_inc(loaded_rest, 16)
            for s_, rows in ((stack_q, a["rows_q"]), (stack_k, a["rows_k"])):
                sp.dma_start(s_[KS:KS + NR, :].rearrange("r (h t) -> r h t", t=S),
                             rows.unsqueeze(1).broadcast_to([NR, RING * HG, S])).then_inc(loaded_att, 16)
            for l in range(2):
                planes_ready, planes_kept = sem(f"planes_ready{l}"), [sem(f"planes_kept{l}_{i}") for i in range(2)]
                stacks_loaded, s2_done = sem(f"stacks_loaded{l}"), sem(f"scores_done{l}")
                u = 0
                for s_ in "kq":
                    for b in range(B):
                        for c in range(C):
                            sp.wait_ge(planes_ready, u + 1)
                            for i in range(2):
                                dst = planes_dram[l, s_][b * GB + 2 * c + i].rearrange("n d j t -> (d j) n t")
                                sp.dma_start(dst, planes[i * 64:(i + 1) * 64, u % 2]).then_inc(planes_kept[u % 2], 16)
                            u += 1
                if l == 1:
                    sp.wait_ge(sem("down0_done"), T)
                    for stack, rows in ((stack_q, a["rows_q"]), (stack_k, a["rows_k"])):
                        sp.dma_start(stack[KS:KS + MP + 1, :].rearrange("r (h t) -> r h t", t=S),
                                     rows[0:MP + 1].unsqueeze(1).broadcast_to([MP + 1, RING * HG, S])
                                     ).then_inc(sem("rows_back"), 16)
                for kept in planes_kept:
                    sp.wait_ge(kept, 16 * u)

                def load_stacks(g):
                    for s_, stack, runs in (("q", stack_q, RUNS_Q), ("k", stack_k, RUNS_K)):
                        for term, plane, n in runs:
                            src = planes_dram[l, s_][bass.ds(g, 1), plane:plane + n].rearrange("g n d j t -> (g n d) (j t)")
                            sp.dma_start(stack[term * DH:(term + n) * DH, bass.ds(slot(g), HG * S)], src
                                         ).then_inc(stacks_loaded, 16)

                def send_maximum(g):
                    sp.wait_ge(sem(f"max_split{l}"), g + 1)
                    apart(sp, "sp")
                    for p in range(MP):
                        sp.dma_start(stack_q[KS + p:KS + p + 1, bass.ds(slot(g), HG * S)], max_planes[0:HG * QT, p, :]
                                     ).then_inc(sem(f"max_sent{l}"), 16)

                def step(g, load=True):
                    sp.wait_ge(stacks_loaded, (g + 3) * (16 * GIVES))
                    apart(sp, "sp")
                    if load:
                        sp.wait_ge(s2_done, 2 * HG * g)
                        apart(sp, "sp")
                        load_stacks(g + 3)
                    sp.wait_ge(sem(f"max_sent{l}"), (g + 2) * (16 * MP))
                    apart(sp, "sp")
                    send_maximum(g + 2)

                load_stacks(0)
                for g in range(1, 3):
                    sp.wait_ge(stacks_loaded, 16 * GIVES * g)
                    load_stacks(g)
                sp.wait_ge(stacks_loaded, 16 * GIVES * 3)
                load_stacks(3)
                send_maximum(0)
                sp.wait_ge(sem(f"max_sent{l}"), 16 * MP)
                send_maximum(1)
                sp.wait_ge(stacks_loaded, 16 * GIVES * 4)
                sp.wait_ge(sem(f"max_sent{l}"), 16 * MP * 2)
                send_maximum(2)
                with sp.Fori(1, G - 3) as g:
                    step(g)
                step(G - 3, load=False)
                if l == 0:
                    sp.wait_ge(sem("normalised0"), 2 * G)
                    sp.dma_start(w1_raw[:], part(a["L0_W1"])).then_inc(sem("w_ffn0"), 16)
                    sp.dma_start(w2_raw[:], part(a["L0_W2"])).then_inc(sem("w_ffn0"), 16)
            sp.wait_ge(sem("normalised1"), 2 * G)
            sp.dma_start(w1_e[:], a["L1_W1"].rearrange("e (c p) n -> p e c n", p=P)).then_inc(sem("w_ffn1"), 16)
            for dst, src in ((w_mo[:], part(a["L1_Wo"])), (b1_e[0:E, :], a["L1_b1"]), (w_router[:], part(a["L1_Wr"])),
                             (bias_mo[:], a["L1_bo"].partition_broadcast(P)),
                             (gamma[:], a["gamma"].partition_broadcast(P)), (beta[:], a["beta"].partition_broadcast(P))):
                sp.dma_start(dst, src).then_inc(sem("w_ffn1"), 16)
            for t in range(T):
                sp.wait_ge(sem("x_final"), t + 1)
                sp.dma_start(out[t * P:(t + 1) * P, :], x[:, t, :]).then_inc(sem("stored"), 16)
            sp.wait_ge(sem("stored"), 16 * T)

        @block.tensor
        def _(pe):
            mm, tr = nc.tensor.matmul, nc.tensor.transpose

            def project(l, s_, u0, src, src_ready):
                for b in range(B):
                    src_ready(b)
                    for c in range(C):
                        u = u0 + b * C + c
                        wait(pe, sem(f"proj_read{l}"), u - 1)
                        for k in range(C):
                            last = mm(ps[u % 2][:], w_qkv[l, s_][:, k, c * P:(c + 1) * P],
                                      src[:, k, b * S:(b + 1) * S], start=(k == 0), stop=(k == C - 1))
                        last.then_inc(sem(f"proj_done{l}"), 1)

            def values(l):
                for v in range(T // 2):
                    wait(pe, sem(f"vals_read{l}"), v - 3)
                    for i in range(2):
                        t = 2 * v + i
                        for k in range(C):
                            last = mm(wide(v)[:, i * D:(i + 1) * D], ctxT[:, k, t * P:(t + 1) * P], w_qkv[l, "v"][:, k, :],
                                      start=(k == 0), stop=(k == C - 1))
                    last.then_inc(sem(f"vals_done{l}"), 1)

            def turn(name, src, before):
                done, read = sem(f"turned_{name}"), sem(f"turned_read_{name}")
                for b in range(B):
                    for c in range(C):
                        u = b * C + c
                        before(b, u)
                        wait(pe, read, u - 3)
                        for i in range(QT):
                            last = tr(wide(u)[:, i * P:(i + 1) * P], src(b * QT + i, c), ident[:])
                        last.then_inc(done, 1)

            def attention(l):
                s1_done, max_done = sem(f"s1_done{l}"), sem(f"max_done{l}")
                s2_done, exp_done = sem(f"scores_done{l}"), sem(f"exp_done{l}")
                pv_done, o_read = sem(f"pv_done{l}"), sem(f"o_read{l}")
                turned, sent = sem(f"max_turned{l}"), sem(f"max_sent{l}")
                rows = KS + (NR if l == 0 else MP + 1)

                def for_maximum(g, j, tiles=range(QT)):
                    if j == 0 and 0 in tiles:
                        wait(pe, sem(f"max_rest{l}"), g)
                    for q in tiles:
                        wait(pe, max_done, (g * HG + j) * QT + q - 1)
                        mm(ps[q % 2][:], stack_q[0:KS, bass.ds(slot(g, j) + q * P, P)],
                           stack_k[0:KS, bass.ds(slot(g, j), S)], start=True, stop=True).then_inc(s1_done, 1)

                def turn_maximum(g):
                    wait(pe, max_done, (g + 1) * HG * QT)
                    tr(ps[0][0:HG * QT, 0:P], row_max[:], ident[:]).then_inc(turned, 1)

                def scores(g, j, half):
                    if j == 0 and half == 0:
                        pe.wait_ge(sent, (g + 1) * (16 * MP))
                    wait(pe, exp_done, (g * HG + j) * 2 + half - 1)
                    for i in range(2):
                        k = 2 * half + i
                        last = mm(pw[half][:, i * S:(i + 1) * S], stack_k[0:rows, bass.ds(slot(g, j) + k * P, P)],
                                  stack_q[0:rows, bass.ds(slot(g, j), S)], start=True, stop=(l == 1),
                                  skip_group_check=True)
                        if l == 0:
                            for p in range(2):
                                last = mm(pw[half][:, i * S + k * P:i * S + (k + 1) * P], rate_eye[:, p, :], behind[:],
                                          start=False, stop=(p == 1), skip_group_check=True)
                    last.then_inc(s2_done, 1)

                def weigh(g, j, tiles=range(QT)):
                    if 0 in tiles:
                        pe.wait_ge(exp_done, (g * HG + j) * 2 + 2)
                        lows_done(pe, l, g, 2 * j + 1)
                        if j % 2 == 0:
                            wait(pe, o_read, 2 * g + j // 2 - 1)
                    for q in tiles:
                        for k in range(QT):
                            for part_, probs_ in enumerate((probs_hi, probs_lo)):
                                last = mm(heads_out[j // 2][:, ((j % 2) * QT + q) * VW:((j % 2) * QT + q + 1) * VW],
                                          probs_[j][:, k * S + q * P:k * S + (q + 1) * P],
                                          vals[:, k, bass.ds(g * HG + j, 1), :],
                                          start=(k == 0 and part_ == 0), stop=(k == QT - 1 and part_ == 1))
                    if QT - 1 in tiles:
                        last.then_inc(pv_done, 1)

                def group(g, first=False, ahead=True):
                    for j in range(HG):
                        for half in range(2):
                            tiles = (2 * half, 2 * half + 1)
                            scores(g, j, half)
                            if ahead:
                                for_maximum(g + 2, j, tiles)
                            if j >= LAG:
                                weigh(g, j - LAG, tiles)
                            elif not first:
                                weigh(g - 1, HG - LAG + j, tiles)
                    if ahead:
                        turn_maximum(g + 2)

                if l == 0:
                    pe.wait_ge(loaded_att, 16 * N_ATT)
                else:
                    pe.wait_ge(sem("rows_back"), 32)
                for g in range(2):
                    pe.wait_ge(sem(f"stacks_loaded{l}"), 16 * GIVES * (g + 1))
                    for j in range(HG):
                        for_maximum(g, j)
                    turn_maximum(g)
                pe.wait_ge(sem(f"vals_low{l}"), T // 2)
                pe.wait_ge(sem(f"stacks_loaded{l}"), 16 * GIVES * 3)
                group(0, first=True)
                with pe.Fori(1, G - 2) as g:
                    pe.wait_ge(sem(f"stacks_loaded{l}"), (g + 3) * (16 * GIVES))
                    group(g)
                group(G - 2, ahead=False)
                group(G - 1, ahead=False)
                for j in range(HG - LAG, HG):
                    weigh(G - 1, j)

            pe.wait_ge(loaded_first, 16 * N_FIRST)
            for l in range(2):
                n = 2 * l
                project(l, "k", 0, ctxT, lambda b: None)
                if l == 1:
                    pe.wait_ge(sem("proj_read1"), 1)
                values(l)
                turn(f"n{n}", lambda t, c: xn[:, t, c * P:(c + 1) * P], lambda b, u, l=l, n=n: (
                    wait(pe, sem(f"vals_read{l}"), min(u + 5, 8)), wait(pe, sem(f"normed{n}"), QT * (b + 1))))
                project(l, "q", B * C, xT, lambda b, n=n: wait(pe, sem(f"turned_read_n{n}"), C * (b + 1)))
                if l == 0:
                    pe.wait_ge(sem("rate_ready"), 3)
                pe.wait_ge(sem(f"proj_read{l}"), 2 * B * C)
                attention(l)
                if l == 0:
                    turn("att", lambda t, c: xn[:, t, c * P:(c + 1) * P], lambda b, u: (wait(pe, sem("exp_done0"), 2 * B * H),
                                                        wait(pe, sem("normalised0"), (b + 1) * GB * 2)))
                    for t in range(T):
                        wait(pe, sem("turned_read_att"), C * (t // QT + 1))
                        wait(pe, sem("oproj_read"), t - 1)
                        for k in range(C):
                            last = mm(ps[t % 2][:, 0:D], xT[:, k, t * P:(t + 1) * P], w_o[:, k, :],
                                      start=(k == 0), stop=(k == C - 1))
                        last.then_inc(sem("oproj_done"), 1)
                    for w in range(2):
                        pe.wait_ge(sem("abs_sum"), w + 1)
                        mm(pm[:, w:w + 1], ones[:], quant[:, w:w + 1], start=True, stop=True).then_inc(sem("gamma_done"), 1)
                    turn("n1", lambda t, c: xn[:, t, c * P:(c + 1) * P],
                         lambda b, u: (wait(pe, sem("turned_read_att"), B * C), wait(pe, sem("normed1"), QT * (b + 1))))
                    pe.wait_ge(sem("w_quant"), 4)
                    pe.wait_ge(sem("oproj_read"), T)
                    for b in range(B + 1):
                        if b < B:
                            pe.wait_ge(sem("turned_read_n1"), C * (b + 1))
                            for f in range(FC):
                                u = b * FC + f
                                wait(pe, sem("hid0_done"), u - 1)
                                for k in range(C):
                                    last = mm(ps[u % 2][:], w1_q[:, k, f * P:(f + 1) * P], xT[:, k, b * S:(b + 1) * S],
                                              start=(k == 0), stop=(k == C - 1))
                                last.then_inc(sem("up0_done"), 1)
                        if b > 0:
                            pe.wait_ge(sem("hid0_done"), b * FC)
                            for q in range(QT):
                                t = (b - 1) * QT + q
                                wait(pe, sem("down0_read"), t - 1)
                                for f in range(FC):
                                    last = mm((po, pm)[t % 2][:, 0:D], hid0[:, (b - 1) % 2, f, q * P:(q + 1) * P], w2_q[:, f, :],
                                              start=(f == 0), stop=(f == FC - 1))
                                last.then_inc(sem("down0_done"), 1)
            pe.wait_ge(sem("w_ffn1"), 16 * 7)
            pe.wait_ge(sem("exp_done1"), 2 * B * H)
            turn("n3", lambda t, c: xn[:, t, c * P:(c + 1) * P], lambda b, u: wait(pe, sem("normed3"), QT * (b + 1)))
            for t in range(T):
                pe.wait_ge(sem("turned_read_n3"), C * (t // QT + 1))
                for k in range(C):
                    last = mm(pm[:, t * E:(t + 1) * E], xT[:, k, t * P:(t + 1) * P], w_router[:, k, :],
                              start=(k == 0), stop=(k == C - 1))
            last.then_inc(sem("logits_done"), 1)
            for b in range(B):
                for q in range(QT):
                    t = b * QT + q
                    pe.wait_ge(sem("masked_done"), t + 1)
                    for e2 in range(2):
                        u = 2 * t + e2
                        wait(pe, sem("masked_read"), u - 3)
                        if u < 4:
                            pe.wait_ge(sem("turned_read_n3"), B * C)
                        for i in range(4):
                            last = tr(wide(u)[:, i * P:(i + 1) * P],
                                      masked_nat[:, t % 2, 2 * e2 + i // C, (i % C) * P:(i % C + 1) * P], ident[:])
                        last.then_inc(sem("masked_turned"), 1)
                if b == 0:
                    pe.wait_ge(sem("routed"), 1)
                    pe.wait_ge(sem("logits_read"), 1)
                wait(pe, sem("hot_read"), b)
                wait(pe, sem("down1_read"), QT * b)
                for q in range(QT):
                    last = tr(pm[0:E, q * P:(q + 1) * P], onehot[:, b * QT + q, :], ident[:])
                last.then_inc(sem("hot_turned"), 1)
                pe.wait_ge(sem("masked_read"), 2 * QT * (b + 1))
                pe.wait_ge(sem("hot_read"), b + 1)
                for f in range(FC):
                    u = b * FC + f
                    wait(pe, sem("hid1_done"), u - 1)
                    mm(ps[u % 2][:], b1_e[0:E, f * P:(f + 1) * P], onehotT[0:E, :], start=True, stop=False)
                    for k in range(E * C):
                        last = mm(ps[u % 2][:], w1_e[:, k // C, k % C, f * P:(f + 1) * P], masked[:, k, :],
                                  start=False, stop=(k == E * C - 1))
                    last.then_inc(sem("up1_done"), 1)
                pe.wait_ge(sem("hid1_done"), (b + 1) * FC)
                for q in range(QT):
                    t = b * QT + q
                    wait(pe, sem("down1_read"), t - 1)
                    if t < 2:
                        pe.wait_ge(sem("hot_read"), 1)
                    for f in range(FC):
                        last = mm((po, pm)[t % 2][:, 0:D], hid1[:, f, q * P:(q + 1) * P], w_mo[:, f, :],
                                  start=(f == 0), stop=(f == FC - 1))
                    last.then_inc(sem("down1_done"), 1)

        @block.scalar
        def _(act):
            do = nc.scalar.activation

            def project_out(l, s_, u0):
                done, read, fulls = sem(f"proj_done{l}"), sem(f"proj_read{l}"), sem(f"full{l}")
                n = B * C
                for i in range(n + 1):
                    u = u0 + i
                    if i < n:
                        act.wait_ge(done, u + 1)
                        wait(act, sem(f"planes_ready{l}"), u - 1)
                        if l == 0:
                            c = u % C
                            ins = do(full[:, u % 2, :], ps[u % 2][:], ACT.Identity,
                                     bias=bias_qk[:, 2 if s_ == "q" else 1, c:c + 1], scale=0.25 if s_ == "q" else 1.0)
                        else:
                            ins = do(full[:, u % 2, :], ps[u % 2][:], ACT.Relu, scale=0.25 if s_ == "q" else 1.0)
                        ins.then_inc(read, 1)
                    if i > 0:
                        act.wait_ge(sem(f"rest{l}"), u)
                        do(planes[:, (u - 1) % 2, 1, :], rest[:, (u - 1) % 2, :], ACT.Copy).then_inc(sem(f"middle{l}"), 1)

            def split_values(l):
                n = T // 2
                for i in range(n + 1):
                    if i < n:
                        act.wait_ge(sem(f"vals_read{l}"), i + 1)
                        do(vals_plane(i, 0), halves(v_full, i), ACT.Copy).then_inc(sem(f"vals_high{l}"), 1)
                    if i > 0:
                        act.wait_ge(sem(f"vals_rest{l}"), i)
                        do(vals_plane(i - 1, 1), halves(v_rest, i - 1), ACT.Copy).then_inc(sem(f"vals_middle{l}"), 1)

            def turned_out(name):
                for b in range(B):
                    for c in range(C):
                        u = b * C + c
                        act.wait_ge(sem(f"turned_{name}"), u + 1)
                        do(xT[:, c, b * S:(b + 1) * S], wide(u), ACT.Copy).then_inc(sem(f"turned_read_{name}"), 1)

            def attention(l):
                s2_done, exp_done, pv_done = sem(f"scores_done{l}"), sem(f"exp_done{l}"), sem(f"pv_done{l}")
                turned = sem(f"max_turned{l}")

                def high_maximum(g):
                    act.wait_ge(turned, g + 1)
                    wait(act, sem(f"max_sent{l}"), g * (16 * MP))
                    do(max_planes[0:HG * QT, 0, :], ps[0][0:HG * QT, 0:P], ACT.Copy, scale=-1.0
                       ).then_inc(sem(f"max_high{l}"), 1)

                def group(g, ahead=True):
                    for j in range(HG):
                        for half in range(2):
                            n = (g * HG + j) * 2 + half
                            act.wait_ge(s2_done, n + 1)
                            if half == 0:
                                wait(act, pv_done, (g - 1) * HG + j + 1)
                                lows_done(act, l, g, 2 * j - 3)
                            cols = slice(half * 2 * S, (half + 1) * 2 * S)
                            do(probs[j % 2][:, cols], pw[half][:], ACT.Exp).then_inc(sem(f"exp_full{l}"), 1)
                            do(probs_hi[j][:, cols], pw[half][:], ACT.Exp).then_inc(exp_done, 1)
                    if ahead:
                        high_maximum(g + 2)

                high_maximum(0)
                high_maximum(1)
                for i in range(2):
                    act.wait_ge(sem(f"planes_kept{l}_{i}"), 2 * 16 * B * C)
                act.wait_ge(sem(f"vals_low{l}"), T // 2)
                group(0)
                with act.Fori(1, G - 2) as g:
                    group(g)
                group(G - 2, ahead=False)
                group(G - 1, ahead=False)

            act.wait_ge(loaded_first, 16 * N_FIRST)
            act.wait_ge(loaded_rest, 16 * N_REST)
            act.wait_ge(sem("prepared"), 1)
            do(gates[:], gates_raw[:], ACT.Tanh).then_inc(sem("gates"), 1)
            for l in range(2):
                if l == 1:
                    act.wait_ge(sem("down0_done"), T)
                project_out(l, "k", 0)
                split_values(l)
                turned_out(f"n{2 * l}")
                project_out(l, "q", B * C)
                attention(l)
                if l == 0:
                    turned_out("att")
                    act.wait_ge(sem("w_ffn0"), 32)
                    for w, raw in enumerate((w1_raw, w2_raw)):
                        do(hid0[:, w].rearrange("p f s -> p (f s)")[:, 0:C * FF], raw[:].rearrange("p c n -> p (c n)"),
                           ACT.Abs, accum_out=quant[:, w:w + 1]).then_inc(sem("abs_sum"), 1)
                    turned_out("n1")
                    act.wait_ge(sem("abs_sum"), 2)
                    for b in range(B):
                        wait(act, sem("down0_done"), QT * (b - 1))
                        for f in range(FC):
                            u = b * FC + f
                            act.wait_ge(sem("up0_done"), u + 1)
                            do(hid0[:, b % 2, f, :], ps[u % 2][:], ACT.Relu, bias=b1_cols[:, f:f + 1]
                               ).then_inc(sem("hid0_done"), 1)
            turned_out("n3")
            for b in range(B):
                wait(act, sem("down1_done"), QT * b)
                for f in range(FC):
                    u = b * FC + f
                    act.wait_ge(sem("up1_done"), u + 1)
                    do(hid1[:, f, :], ps[u % 2][:], ACT.Gelu).then_inc(sem("hid1_done"), 1)

        @block.gpsimd
        def _(pool):
            nc.gpsimd.memset(minus_half[:], -0.5).then_inc(sem("half_ready"), 1)
            pool.wait_ge(sem("half_ready"), 1)
            v = nc.gpsimd

            def roots(n, t0=0, t1=T):
                pool.wait_ge(sem("var_ready"), n)
                v.tensor_tensor(root[:, t0:t1], var_eps[:, t0:t1], minus_half[:, t0:t1], ALU.pow
                                ).then_inc(sem("root_ready"), 1)

            def split_values(l):
                n = T // 2
                for i in range(n + 1):
                    if i < n:
                        pool.wait_ge(sem(f"vals_high{l}"), i + 1)
                        v.tensor_tensor(halves(v_rest, i), halves(v_full, i), vals_plane(i, 0), ALU.subtract
                                        ).then_inc(sem(f"vals_rest{l}"), 1)
                    if i > 0:
                        pool.wait_ge(sem(f"vals_middle{l}"), i)
                        v.tensor_tensor(vals_plane(i - 1, 2), halves(v_rest, i - 1), vals_plane(i - 1, 1), ALU.subtract
                                        ).then_inc(sem(f"vals_low{l}"), 1)

            def attention(l):
                def low_maximum(g):
                    n = HG * QT
                    pool.wait_ge(sem(f"max_rest{l}"), g + 1)
                    apart(pool, "pool")
                    v.tensor_copy(max_planes[0:n, 1, :], max_rest[0:n, :]).then_inc(sem(f"max_middle{l}"), 1)
                    pool.wait_ge(sem(f"max_middle{l}"), g + 1)
                    v.tensor_tensor(max_planes[0:n, 2, :], max_rest[0:n, :], max_planes[0:n, 1, :], ALU.subtract
                                    ).then_inc(sem(f"max_split{l}"), 1)

                def group(g, ahead=True):
                    for n in LOW_POOL:
                        low_part(pool, v, l, g, n).then_inc(sem(f"low_pool{l}"), 1)
                    if ahead:
                        low_maximum(g + 2)

                low_maximum(0)
                low_maximum(1)
                group(0)
                with pool.Fori(1, G - 2) as g:
                    group(g)
                group(G - 2, ahead=False)
                group(G - 1, ahead=False)

            roots(1)
            split_values(0)
            attention(0)
            roots(2)
            roots(3)
            split_values(1)
            attention(1)
            roots(4)
            for t in range(T):
                roots(5 + t, t, t + 1)

        @block.vector
        def _(dve):
            v = nc.vector

            rooted = [0]

            def inverse_root(n, t0, t1, eps):
                w, r, h, y1 = (z[:, t0:t1] for z in (var_eps, root, newton, rstd))
                rooted[0] += 1
                st, k = sem("newton_step"), 4 * rooted[0] - 4
                v.tensor_scalar(w, meanvar[:, t0:t1, 1], eps, None, ALU.add).then_inc(sem("var_ready"), 1)
                dve.wait_ge(sem("root_ready"), rooted[0])
                v.tensor_tensor(h, r, r, ALU.mult).then_inc(st, 1)
                dve.wait_ge(st, k + 1)
                v.tensor_tensor(h, h, w, ALU.mult).then_inc(st, 1)
                dve.wait_ge(st, k + 2)
                v.tensor_scalar(h, h, -0.5, 1.5, ALU.mult, ALU.add).then_inc(st, 1)
                dve.wait_ge(st, k + 3)
                v.tensor_tensor(y1, h, r, ALU.mult).then_inc(st, 1)
                dve.wait_ge(st, k + 4)

            def norm_stats(n, eps):
                s_, ag = sem(f"stats{n}"), sem(f"aggr{n}")
                with dve.Fori(0, T) as t:
                    v.bn_stats(stats[:, bass.ds(t, 1), :], x[:, bass.ds(t, 1), :]).then_inc(s_, 1)
                dve.wait_ge(s_, T)
                for t in range(T):
                    v.bn_aggr(meanvar[:, t, :], stats[:, t, :]).then_inc(ag, 1)
                dve.wait_ge(ag, T)
                inverse_root(n, 0, T, eps)

            def norm(n):
                norm_stats(n, 1e-5)
                for t in range(T):
                    v.tensor_scalar(xn[:, t, :], x[:, t, :], meanvar[:, t, 0:1], rstd[:, t:t + 1],
                                    ALU.subtract, ALU.mult).then_inc(sem(f"normed{n}"), 1)

            def split(l, u0):
                hi, rs = sem(f"high{l}"), sem(f"rest{l}")
                n = B * C
                for i in range(n + 1):
                    u = u0 + i
                    if i < n:
                        dve.wait_ge(sem(f"proj_read{l}"), u + 1)
                        wait(dve, sem(f"planes_kept{l}_{u % 2}"), 2 * 16 * (u // 2))
                        v.tensor_copy(planes[:, u % 2, 0, :], full[:, u % 2, :]).then_inc(hi, 1)
                        dve.wait_ge(hi, u + 1)
                        v.tensor_tensor(rest[:, u % 2, :], full[:, u % 2, :], planes[:, u % 2, 0, :],
                                        ALU.subtract).then_inc(rs, 1)
                    if i > 0:
                        dve.wait_ge(sem(f"middle{l}"), u)
                        v.tensor_tensor(planes[:, (u - 1) % 2, 2, :], rest[:, (u - 1) % 2, :], planes[:, (u - 1) % 2, 1, :],
                                        ALU.subtract).then_inc(sem(f"planes_ready{l}"), 1)

            def values(l):
                for k in range(T // 2):
                    dve.wait_ge(sem(f"vals_done{l}"), k + 1)
                    wait(dve, sem(f"vals_low{l}"), k - 1)
                    src = wide(k).rearrange("p (n d) -> p n d", n=2)
                    if l == 0:
                        ins = v.tensor_tensor(v_full[:, k % 2], src, bias_v[:].unsqueeze(1).broadcast_to([P, 2, D]), ALU.add)
                    else:
                        ins = v.tensor_scalar(v_full[:, k % 2], src, 0.0, None, ALU.max)
                    ins.then_inc(sem(f"vals_read{l}"), 1)

            def attention(l):
                s1_done, max_done = sem(f"s1_done{l}"), sem(f"max_done{l}")
                pv_done, o_read, turned = sem(f"pv_done{l}"), sem(f"o_read{l}"), sem(f"max_turned{l}")

                def maxima(g, j):
                    if j == 0:
                        wait(dve, turned, g)
                    for q in range(QT):
                        dst = row_max[:, j * QT + q:j * QT + q + 1]
                        dve.wait_ge(s1_done, (g * HG + j) * QT + q + 1)
                        if l == 0:
                            apart(dve, "dve")
                            at = (QT - 1 - q) * P
                            v.tensor_tensor_reduce(biased[:, q % 2, :], ps[q % 2][:], time_bias[:, at:at + S], 1.0, LOWEST,
                                                   ALU.add, ALU.max, dst).then_inc(max_done, 1)
                        else:
                            v.tensor_reduce(dst, ps[q % 2][:], AX, ALU.max).then_inc(max_done, 1)

                def rest_maximum(g):
                    n = HG * QT
                    dve.wait_ge(sem(f"max_high{l}"), g + 1)
                    wait(dve, sem(f"max_split{l}"), g)
                    v.scalar_tensor_tensor(out=max_rest[0:n, :], in0=ps[0][0:n, 0:P], scalar=-1.0, in1=max_planes[0:n, 0, :],
                                           op0=ALU.mult, op1=ALU.subtract).then_inc(sem(f"max_rest{l}"), 1)

                def normalise(g, i):
                    dve.wait_ge(pv_done, g * HG + 2 * i + 2)
                    wait(dve, sem(f"normalised{l}"), 2 * g + i)
                    o = heads_out[i][:, 0:2 * QT * VW].rearrange("p (n w) -> p n w", w=VW)
                    v.reciprocal(recip[:], o[:, :, VP * DH]).then_inc(sem(f"recip{l}"), 1)
                    planes_last = o[:, :, 0:VP * DH].rearrange("p n (v d) -> p n d v", v=VP)
                    v.tensor_reduce(summed[:], planes_last, AX, ALU.add).then_inc(o_read, 1)
                    dve.wait_ge(sem(f"recip{l}"), 2 * g + i + 1)
                    dve.wait_ge(o_read, 2 * g + i + 1)
                    by_pair = xn[:].rearrange("p (b q) (n i j d) -> p b n i q j d", q=QT, n=GB, i=2, d=DH)
                    dst = by_pair[:, bass.ds((g >> 2) & (B - 1), 1), bass.ds(g & (GB - 1), 1), i].rearrange("p b n q j d -> p (b n q) j d")
                    v.tensor_tensor(dst, summed[:].rearrange("p (j q) d -> p q j d", q=QT),
                                    recip[:].rearrange("p (j q) -> p q j", q=QT).unsqueeze(3).broadcast_to([P, QT, 2, DH]),
                                    ALU.mult).then_inc(sem(f"normalised{l}"), 1)

                def group(g, first=False, ahead=True):
                    for j in range(HG):
                        if ahead:
                            maxima(g + 2, j)
                        for n in LOW_DVE:
                            if n // 2 == j:
                                low_part(dve, v, l, g, n).then_inc(sem(f"low_dve{l}"), 1)
                        if j % 2 == 0 and not first:
                            normalise(g - 1, j // 2)
                    if ahead:
                        rest_maximum(g + 2)

                for g in range(2):
                    for j in range(HG):
                        maxima(g, j)
                    rest_maximum(g)
                group(0, first=True)
                with dve.Fori(1, G - 2) as g:
                    group(g)
                group(G - 2, ahead=False)
                group(G - 1, ahead=False)
                for i in range(2):
                    normalise(G - 1, i)
                dve.wait_ge(sem(f"normalised{l}"), 2 * G)

            def quantise():
                dve.wait_ge(sem("gamma_done"), 2)
                v.tensor_scalar(quant[:, 2:4], pm[:, 0:2], 1.0 / (D * FF), 1e-5, ALU.mult, ALU.add).then_inc(sem("q_step"), 1)
                dve.wait_ge(sem("q_step"), 1)
                v.tensor_scalar(quant[:, 4:6], quant[:, 2:4], 0.5, None, ALU.mult).then_inc(sem("q_step"), 1)
                v.tensor_scalar(quant[:, 6:8], quant[:, 2:4], -0.5, None, ALU.mult).then_inc(sem("q_step"), 1)
                dve.wait_ge(sem("q_step"), 3)
                for w, (raw, q) in enumerate(((w1_raw, w1_q), (w2_raw, w2_q))):
                    v.tensor_scalar(q[:], raw[:], quant[:, 6 + w:7 + w], None, ALU.is_lt).then_inc(sem("w_quant"), 1)
                    dve.wait_ge(sem("w_quant"), 2 * w + 1)
                    v.scalar_tensor_tensor(out=q[:], in0=raw[:], scalar=quant[:, 4 + w:5 + w], in1=q[:],
                                           op0=ALU.is_gt, op1=ALU.subtract).then_inc(sem("w_quant"), 1)

            def add_gated(name, t, src, bias, gate):
                v.tensor_tensor(tmp[:, t % 2, :], src, bias, ALU.add).then_inc(sem(name), 1)
                dve.wait_ge(sem(name), t + 1)
                return v.scalar_tensor_tensor(out=x[:, t, :], in0=tmp[:, t % 2, :], scalar=gates[:, gate:gate + 1],
                                              in1=x[:, t, :], op0=ALU.mult, op1=ALU.add)

            v.memset(ones[:], 1.0).then_inc(sem("dve_const"), 1)
            v.memset(vals[:, :, :, VP * DH:VW], 1.0).then_inc(sem("dve_const"), 1)
            dve.wait_ge(loaded_first, 16 * N_FIRST)
            v.tensor_scalar(bias_qk[:, 2, :], bias_qk[:, 0, :], 0.25, None, ALU.mult).then_inc(sem("prepared"), 1)
            norm(0)
            dve.wait_ge(loaded_rest, 16 * N_REST)
            v.tensor_copy(behind[:], behind_raw[:]).then_inc(sem("rate_ready"), 1)
            v.tensor_scalar(rate_eye[:, 0, :], ident[:], float(TIME_RATE), None, ALU.mult).then_inc(sem("rate_ready"), 1)
            dve.wait_ge(sem("rate_ready"), 2)
            v.scalar_tensor_tensor(out=rate_eye[:, 1, :], in0=ident[:], scalar=float(TIME_RATE), in1=rate_eye[:, 0, :],
                                   op0=ALU.mult, op1=ALU.subtract).then_inc(sem("rate_ready"), 1)
            dve.wait_ge(sem("rate_ready"), 3)

            for l in range(2):
                if l == 1:
                    norm(2)
                split(l, 0)
                values(l)
                split(l, B * C)
                attention(l)
                if l == 0:
                    dve.wait_ge(sem("gates"), 1)
                    for t in range(T):
                        dve.wait_ge(sem("oproj_done"), t + 1)
                        ins = add_gated("oproj_tmp", t, ps[t % 2][:, 0:D], bias_o[:], 0)
                        ins.then_inc(sem("oproj_read"), 1)
                    dve.wait_ge(sem("oproj_read"), T)
                    dve.wait_ge(sem("turned_att"), B * C)
                    norm(1)
                    dve.wait_ge(sem("w_ffn0"), 32)
                    quantise()
                    for t in range(T):
                        dve.wait_ge(sem("down0_done"), t + 1)
                        ins = add_gated("down0_tmp", t, (po, pm)[t % 2][:, 0:D], bias_2[:], 2)
                        ins.then_inc(sem("down0_read"), 1)
                    dve.wait_ge(sem("down0_read"), T)
            for t in range(T):
                v.scalar_tensor_tensor(out=x[:, t, :], in0=xn[:, t, :], scalar=gates[:, 1:2], in1=x[:, t, :],
                                       op0=ALU.mult, op1=ALU.add).then_inc(sem("x_att1"), 1)
            dve.wait_ge(sem("x_att1"), T)
            norm(3)
            dve.wait_ge(sem("logits_done"), 1)
            v.tensor_copy(logits[:], pm[:, 0:T * E].rearrange("p (t e) -> p t e", e=E)).then_inc(sem("logits_read"), 1)
            dve.wait_ge(sem("logits_read"), 1)
            rt = sem("route_step")
            v.tensor_reduce(top[:], logits[:], AX, ALU.max).then_inc(rt, 1)
            dve.wait_ge(rt, 1)
            v.tensor_tensor(onehot[:], logits[:], top[:].unsqueeze(2).broadcast_to([P, T, E]), ALU.is_equal).then_inc(rt, 1)
            dve.wait_ge(rt, 2)
            v.tensor_tensor(logits[:], onehot[:], order[:].unsqueeze(1).broadcast_to([P, T, E]), ALU.mult).then_inc(rt, 1)
            dve.wait_ge(rt, 3)
            v.tensor_reduce(top[:], logits[:], AX, ALU.max).then_inc(rt, 1)
            dve.wait_ge(rt, 4)
            v.tensor_tensor(onehot[:], logits[:], top[:].unsqueeze(2).broadcast_to([P, T, E]), ALU.is_equal).then_inc(sem("routed"), 1)
            dve.wait_ge(sem("routed"), 1)
            dve.wait_ge(sem("exp_done1"), 2 * B * H)
            dve.wait_ge(sem("w_ffn1"), 16 * 7)

            def mask(t):
                wait(dve, sem("masked_turned"), 2 * (t - 1))
                for e in range(E):
                    ins = v.tensor_scalar(masked_nat[:, t % 2, e, :], xn[:, t, :], onehot[:, t, e:e + 1], None, ALU.mult)
                ins.then_inc(sem("masked_done"), 1)

            for b in range(B):
                for q in range(QT + 1):
                    t = b * QT + q
                    if q < QT:
                        mask(t)
                    if q > 0:
                        wait(dve, sem("up1_done"), b * FC)
                        for e2 in range(2):
                            u = 2 * (t - 1) + e2
                            dve.wait_ge(sem("masked_turned"), u + 1)
                            v.tensor_copy(masked[:, 4 * e2:4 * e2 + 4, (q - 1) * P:q * P],
                                          wide(u).rearrange("p (n t) -> p n t", t=P)).then_inc(sem("masked_read"), 1)
                dve.wait_ge(sem("hot_turned"), b + 1)
                v.tensor_copy(onehotT[0:E, :], pm[0:E, :]).then_inc(sem("hot_read"), 1)
                for q in range(QT):
                    t = b * QT + q
                    dve.wait_ge(sem("down1_done"), t + 1)
                    st = sem("tail")
                    base = 7 * t
                    yt, k = y[:, t % 2, :], t % 2
                    v.tensor_tensor(yt, (po, pm)[t % 2][:, 0:D], bias_mo[:], ALU.add).then_inc(sem("down1_read"), 1)
                    dve.wait_ge(sem("down1_read"), t + 1)
                    v.tensor_tensor(yt, yt, xn[:, t, :], ALU.add).then_inc(st, 1)
                    dve.wait_ge(st, base + 1)
                    v.bn_stats(stats[:, t, :], yt).then_inc(st, 1)
                    dve.wait_ge(st, base + 2)
                    v.bn_aggr(meanvar[:, t, :], stats[:, t, :]).then_inc(st, 1)
                    dve.wait_ge(st, base + 3)
                    inverse_root(4, t, t + 1, 1e-12)
                    v.tensor_scalar(yt, yt, meanvar[:, t, 0:1], rstd[:, t:t + 1], ALU.subtract, ALU.mult).then_inc(st, 1)
                    dve.wait_ge(st, base + 4)
                    v.tensor_tensor(yt, yt, gamma[:], ALU.mult).then_inc(st, 1)
                    dve.wait_ge(st, base + 5)
                    v.tensor_tensor(yt, yt, beta[:], ALU.add).then_inc(st, 2)
                    dve.wait_ge(st, base + 7)
                    v.scalar_tensor_tensor(out=x[:, t, :], in0=yt, scalar=gates[:, 3:4], in1=x[:, t, :],
                                           op0=ALU.mult, op1=ALU.add).then_inc(sem("x_final"), 1)


def kernel(**inputs):
    import concourse.bacc as _bacc
    from concourse.bass_utils import run_bass_kernel_spmd as _run

    def host(name):
        return np.asarray(inputs[name])

    def cols(v):
        return v.reshape(-1, P).T

    def grouped(v):
        return v.reshape(GB, HG, DH, -1).transpose(0, 2, 1, 3).reshape(v.shape)

    lay = {
        "x": host("x").reshape(B * S, D), "ctxT": host("ctx_1024").reshape(B * S, D).T,
        "gates": np.concatenate([host("g_xattn"), host("g_ffn")]),
        "L0_Wq": grouped(host("L0_xattn_Wq")).T, "L0_Wk": grouped(host("L0_xattn_Wk")).T, "L0_Wv": host("L0_xattn_Wv").T,
        "L0_Wo": host("L0_xattn_Wo").T, "L0_bq": cols(grouped(host("L0_xattn_bq"))), "L0_bk": cols(grouped(host("L0_xattn_bk"))),
        "L0_bv": host("L0_xattn_bv"), "L0_bo": host("L0_xattn_bo"),
        "L0_W1": host("L0_ffn_W1").T, "L0_b1": cols(host("L0_ffn_b1")), "L0_W2": host("L0_ffn_W2").T,
        "L0_b2": host("L0_ffn_b2"),
        "L1_Wq": grouped(host("L1_xattn_Wq")).T, "L1_Wk": grouped(host("L1_xattn_Wk")).T, "L1_Wv": host("L1_xattn_Wv").T,
        "L1_Wr": host("L1_ffn_W_router"), "L1_W1": host("L1_ffn_W1"), "L1_b1": host("L1_ffn_b1"),
        "L1_Wo": host("L1_ffn_Wo"), "L1_bo": host("L1_ffn_bo"), "gamma": host("L1_ffn_ln_gamma"),
        "beta": host("L1_ffn_ln_beta"),
    }
    import ml_dtypes
    tables = constants()
    for name in ("rows_q", "rows_k"):
        tables[name] = tables[name].astype(ml_dtypes.bfloat16)
    lay.update(tables)
    nc = _bacc.Bacc("TRN2", target_bir_lowering=False, num_devices=1)
    arrays, args = {}, {}
    for name, v in lay.items():
        v = np.ascontiguousarray(v)
        arrays[f"in_{name}"] = v
        args[name] = nc.dram_tensor(f"in_{name}", v.shape, mybir.dt.from_np(v.dtype), kind="ExternalInput").ap()
    out = nc.dram_tensor("out_x", (B * S, D), F32, kind="ExternalOutput").ap()
    gated_blocks_program(nc, args, out)
    r = _run(nc, [arrays], core_ids=[0])
    return r.results[0]["out_x"].reshape(B, S, D)
```

```python
from contextlib import ExitStack

import numpy as np
import concourse.bass as bass
from concourse import mybir

ALU = mybir.AluOpType
ACT = mybir.ActivationFunctionType
AX = mybir.AxisListType.X
F32 = mybir.dt.float32
F32R = mybir.dt.float32r
BF16 = mybir.dt.bfloat16
F16 = mybir.dt.float16

P = 128
B, S, D = 4, 512, 256
T = B * S // P
QT = S // P
H, DH = 16, 16
C = D // P
FF = 1024
FC = FF // P
E = 4
HG = 4
G = B * H // HG
GB = H // HG
RING = 4
VP = 3
VW = VP * DH + 4
TERMS = ((0, 0), (1, 1), (0, 1), (0, 2), (1, 0), (2, 0))
RUNS_Q = ((0, 0, 2), (2, 0, 1), (3, 0, 1), (4, 1, 2))
RUNS_K = ((0, 0, 2), (2, 1, 2), (4, 0, 1), (5, 0, 1))
GIVES = len(RUNS_Q) + len(RUNS_K)
KS = len(TERMS) * DH
MP = 3
LOWS_DVE = (0, 1)
LOWS_POOL = (2, 3)
SCALE_LOG = 6.9375
LAG = 2
UNITS = 4
VALS = 3
LOWEST = -3.0e38
LOW_DVE = (2, 6)
LOW_POOL = tuple(n for n in range(2 * HG) if n not in LOW_DVE)
TIME_RATE = np.float32(-0.1)


def bf16_planes(a, n):
    out, rest = [], a.astype(np.float32)
    for _ in range(n):
        hi = (rest.view(np.uint32) & np.uint32(0xFFFF0000)).view(np.float32)
        out.append(hi)
        rest = (rest - hi).astype(np.float32)
    return out


def constants():
    t = np.arange(S)
    rate_t = (np.float32(0.1) * (t - S // 2).astype(np.float32)).astype(np.float32)
    tile = t // P
    sign = np.where(tile[None, :] >= np.arange(QT)[:, None], 1.0, -1.0).astype(np.float32)
    here = (tile[None, :] == np.arange(QT)[:, None]).astype(np.float32)
    q_rows, k_rows = [np.zeros(S, np.float32)] * MP, [np.ones(S, np.float32)] * (MP + 1)
    q_rows.append(np.full(S, SCALE_LOG, np.float32))
    planes = bf16_planes(rate_t, 3)
    for k in range(QT):
        for p in planes:
            q_rows.append(-p * sign[k])
            k_rows.append(here[k])
            q_rows.append(sign[k])
            k_rows.append(here[k] * p)
    p = np.arange(P)
    behind = 2.0 * np.maximum(p[:, None] - p[None, :], 0)
    bias = TIME_RATE * np.abs(np.arange(2 * S - P)[None, :] - p[:, None] - (S - P)).astype(np.float32)
    return {
        "rows_q": np.stack(q_rows).astype(np.float32),
        "rows_k": np.stack(k_rows).astype(np.float32),
        "behind": behind.astype(np.float32),
        "time_bias": bias.astype(np.float32),
        "ident": np.eye(P, dtype=np.float32),
        "order": np.broadcast_to(np.arange(E, 0, -1, dtype=np.float32), (P, E)).copy(),
    }


NR = MP + 1 + 6 * QT
HOT = 32 + E
PARTS = ("hi", "lo")
PRODUCTS = ((0, 0), (0, 1), (1, 0))


def gated_blocks_program(nc, a, out):
    with ExitStack() as ctx:
        def dram(name, shape, dt):
            return nc.dram_tensor(name, shape, dt, kind="Internal").ap()

        def sb(name, shape, dt=F32, scope=ctx):
            return scope.enter_context(nc.sbuf_tensor(name, shape, dt))

        planes_dram = {(l, s): dram(f"planes_{l}_{s}", [G, 3, DH, HG, S], BF16) for l in range(2) for s in "qk"}

        x = sb("x", [P, T, D])
        xn = sb("xn", [P, T, D])
        ident = sb("ident_sb", [P, P])
        bias_mo = sb("bias_mo", [P, D])
        gamma = sb("gamma", [P, D])
        beta = sb("beta", [P, D])
        bias_qk = sb("bias_qk", [P, 3, C])
        b1_cols = sb("b1_cols", [P, FC])
        gates_raw = sb("gates_raw", [P, 4])
        gates = sb("gates", [P, 4])
        stats = sb("stats", [P, T, 6])
        meanvar = sb("meanvar", [P, T, 2])
        rstd = sb("rstd", [P, T])
        var_eps = sb("var_eps", [P, T])
        root = sb("root", [P, T])
        newton = sb("newton", [P, T])
        minus_half = sb("minus_half", [P, T])
        order = sb("order_sb", [P, E])
        w_router = sb("w_router", [P, C, E])
        quant = sb("quant", [P, 8])
        logits = sb("logits", [P, QT, E])
        top = sb("top", [P, QT])
        onehot = sb("onehot", [P, QT, HOT])

        with ExitStack() as pro:
            ctxT = sb("ctxT", [P, C, B * S], F32, pro)
            w_qkv = {s_: sb(f"w_{s_}", [P, C, D], F32, pro) for s_ in "qkv"}
            w_o = sb("w_o", [P, C, D], F32, pro)
            bias_v = sb("bias_v", [P, D], F32, pro)
            bias_o = sb("bias_o", [P, D], F32, pro)
            bias_2 = sb("bias_2", [P, D], F32, pro)
            tmp = sb("tmp", [P, 2, D], F32, pro)
            ones = sb("ones", [P, P], F32, pro)
            with ExitStack() as rows_:
                xT = sb("xT", [P, C, B * S], F32, rows_)
            with ExitStack() as rows_:
                xT_hi = sb("xT_hi", [P, 2, C, S], F32R, rows_)
                xT_lo = sb("xT_lo", [P, 2, C, S], F32R, rows_)
        x3 = sb("x3", [P, C, S])
        x3_parts = [sb("x3_hi", [P, C, S], F32R)]
        with ExitStack() as moe:
            w1_e_raw = sb("w1_e_raw", [P, E, C, FF], F32, moe)
            w_mo_raw = sb("w_mo_raw", [P, FC, D], F32, moe)
        x3_parts.append(sb("x3_lo", [P, C, S], F32R))
        onehotT = sb("onehotT", [P, 2, S], F32R)
        masked = [sb(f"masked_{h}", [P, E, C, S], F32R) for h in PARTS]

        with ExitStack() as att:
            time_bias = sb("time_bias_sb", [P, 2 * S - P], F32, att)
            biased = sb("biased", [P, 2, S], BF16, att)
            behind_raw = sb("behind_raw", [P, P], F32, att)
            behind = sb("behind_sb", [P, P], F32R, att)
            rate_eye = sb("rate_eye", [P, 2, P], F32R, att)
            row_max = sb("row_max", [P, HG * QT], F32, att)
            max_planes = sb("max_planes", [P, MP, P], BF16, att)
            max_rest = sb("max_rest", [P, P], F32, att)
            recip = sb("recip", [P, 2 * QT], F32, att)
            summed = sb("summed", [P, 2 * QT, DH], F32, att)
            stack_q = sb("stack_q", [P, RING * HG * S], BF16, att)
            stack_k = sb("stack_k", [P, RING * HG * S], BF16, att)
            with ExitStack() as s1:
                full = sb("full", [P, 2, S], F32, s1)
                rest = sb("rest", [P, 2, S], F32, s1)
                planes = sb("planes", [P, UNITS, 3, S], BF16, s1)
                v_full = sb("v_full", [P, VALS, 2, D], F32, s1)
                v_rest = sb("v_rest", [P, 2, 2, D], F32, s1)
            probs = [sb(f"probs{i}", [P, QT * S], F32, att) for i in range(2)]
            probs_hi = [sb(f"probs_hi{i}", [P, QT * S], F16, att) for i in range(HG)]
            probs_lo = [sb(f"probs_lo{i}", [P, QT * S], F16, att) for i in range(HG)]
            vals = sb("vals", [P, QT, B * H, VW], BF16, att)
        with ExitStack() as ffn:
            with ExitStack() as raw_:
                w1_raw = sb("w1_raw", [P, C, FF], F32, raw_)
                w2_raw = sb("w2_raw", [P, FC, D], F32, raw_)
                w_abs = sb("w_abs", [P, C * FF], F32, raw_)
            hid0 = {}
            for slot_ in (1, 0):
                for h in PARTS:
                    hid0[slot_, h] = sb(f"hid0_{h}{slot_}", [P, FC, S], F32R, ffn)
            hid0_full = sb("hid0_full", [P, 4, S], F32, ffn)
            w1_q = sb("w1_q", [P, C, FF], F32R, ffn)
            w2_q = sb("w2_q", [P, FC, D], F32R, ffn)
        with ExitStack() as moe:
            w1_parts = [sb(f"w1_{h}", [P, E, C, FF], F32R, moe) for h in PARTS]
            w_mo_parts = [sb(f"w_mo_{h}", [P, FC, D], F32R, moe) for h in PARTS]
            b1_parts = sb("b1_parts", [P, FF], F32R, moe)
            select = sb("select", [P, E, P], F32R, moe)
            with ExitStack() as raw_:
                b1_raw = sb("b1_raw", [P, FF], F32, raw_)
            hid1_full = sb("hid1_full", [P, 2, S], F32, moe)
            hid1 = [sb(f"hid1_{h}", [P, FC, S], F32R, moe) for h in PARTS]

        ps = [ctx.enter_context(nc.psum_tensor(f"ps_a{i}", [P, S], F32)) for i in range(2)]
        pw = [ctx.enter_context(nc.psum_tensor(f"ps_wide{i}", [P, 2 * S], F32)) for i in range(2)]
        po = ctx.enter_context(nc.psum_tensor("ps_out", [P, S], F32))
        pm = ctx.enter_context(nc.psum_tensor("ps_misc", [P, S], F32))
        heads_out = (po, pm)

        def wide(k):
            return pw[(k // 2) % 2][:, (k % 2) * S:(k % 2) * S + S]

        def vals_bank(v):
            return wide(v)

        sems = {}

        def sem(name):
            if name not in sems:
                sems[name] = ctx.enter_context(nc.semaphore(name))
            return sems[name]

        def wait(eng, s, v):
            if not isinstance(v, int) or v > 0:
                eng.wait_ge(s, v)

        def apart(eng, name):
            eng.sem_inc(sem(f"apart_{name}"), 1)

        loaded_keys, loaded_values, loaded_rows = sem("loaded_keys"), sem("loaded_values"), sem("loaded_rows")
        loaded_rest, loaded_att = sem("loaded_rest"), sem("loaded_att")
        N_KEYS, N_VALUES, N_ROWS, N_REST, N_ATT = 4, 2, 3, 8, 2
        block = ctx.enter_context(nc.Block())

        def part(v):
            return v.rearrange("(c p) n -> p c n", p=P)

        def slot(g, j=0):
            return ((g & (RING - 1)) * HG + j) * S

        def vals_plane(i, p):
            b, q = divmod(2 * i, QT)
            return vals[:, q:q + 2, b * H:(b + 1) * H, p * DH:(p + 1) * DH]

        def halves(t, i):
            return t[:, i % (VALS if t is v_full else 2)].rearrange("p n (h d) -> p n h d", d=DH)

        def planes_left(eng, l, n):
            for i in range(UNITS):
                wait(eng, sem(f"planes_kept{l}_{i}"), 2 * 16 * ((n - i + UNITS - 1) // UNITS))

        def lows_done(eng, l, g, n):
            for name, own in (("pool", LOW_POOL), ("dve", LOW_DVE)):
                wait(eng, sem(f"low_{name}{l}"), g * len(own) + sum(m <= n for m in own) - sum(m > n + 2 * HG for m in own))

        def low_part(eng, ops, l, g, n):
            j, half = divmod(n, 2)
            eng.wait_ge(sem(f"exp_done{l}"), g * (2 * HG) + n + 1)
            cols = slice(half * 2 * S, (half + 1) * 2 * S)
            return ops.tensor_tensor(probs_lo[j][:, cols], probs[j % 2][:, cols], probs_hi[j][:, cols], ALU.subtract)

        @block.sync
        def _(sp):
            for signal, moves in (
                (loaded_keys, ((w_qkv["k"][:], part(a["L0_Wk"])), (bias_qk[:, 0, :], a["L0_bq"]), (bias_qk[:, 1, :], a["L0_bk"]),
                               (ctxT[:], part(a["ctxT"])))),
                (loaded_values, ((w_qkv["v"][:], part(a["L0_Wv"])), (bias_v[:], a["L0_bv"].partition_broadcast(P)))),
                (loaded_rows, ((x[:], a["x"].rearrange("(t p) d -> p t d", p=P)), (ident[:], a["ident"]),
                               (w_qkv["q"][:], part(a["L0_Wq"])))),
            ):
                for dst, src in moves:
                    sp.dma_start(dst, src).then_inc(signal, 16)
            for dst, src in (
                (w_o[:], part(a["L0_Wo"])), (gates_raw[:], a["gates"].partition_broadcast(P)),
                (bias_o[:], a["L0_bo"].partition_broadcast(P)), (bias_2[:], a["L0_b2"].partition_broadcast(P)),
                (b1_cols[:], a["L0_b1"]), (time_bias[:], a["time_bias"]),
                (behind_raw[:], a["behind"]), (order[:], a["order"]),
            ):
                sp.dma_start(dst, src).then_inc(loaded_rest, 16)
            for s_, rows in ((stack_q, a["rows_q"]), (stack_k, a["rows_k"])):
                sp.dma_start(s_[KS:KS + NR, :].rearrange("r (h t) -> r h t", t=S),
                             rows.unsqueeze(1).broadcast_to([NR, RING * HG, S])).then_inc(loaded_att, 16)
            for l in range(2):
                planes_ready, planes_kept = sem(f"planes_ready{l}"), [sem(f"planes_kept{l}_{i}") for i in range(UNITS)]
                stacks_loaded, s2_done = sem(f"stacks_loaded{l}"), sem(f"scores_done{l}")
                def store_planes(s_, b):
                    for c in range(C):
                        u = ((s_ == "q") * B + b) * C + c
                        sp.wait_ge(planes_ready, u + 1)
                        for i in range(2):
                            dst = planes_dram[l, s_][b * GB + 2 * c + i].rearrange("n d j t -> (d j) n t")
                            sp.dma_start(dst, planes[i * 64:(i + 1) * 64, u % UNITS]).then_inc(planes_kept[u % UNITS], 16)

                def load_stacks(g):
                    for s_, stack, runs in (("q", stack_q, RUNS_Q), ("k", stack_k, RUNS_K)):
                        for term, plane, n in runs:
                            src = planes_dram[l, s_][bass.ds(g, 1), plane:plane + n].rearrange("g n d j t -> (g n d) (j t)")
                            sp.dma_start(stack[term * DH:(term + n) * DH, bass.ds(slot(g), HG * S)], src
                                         ).then_inc(stacks_loaded, 16)

                def send_maximum(g):
                    sp.wait_ge(sem(f"max_split{l}"), g + 1)
                    apart(sp, "sp")
                    for p in range(MP):
                        sp.dma_start(stack_q[KS + p:KS + p + 1, bass.ds(slot(g), HG * S)], max_planes[0:HG * QT, p, :]
                                     ).then_inc(sem(f"max_sent{l}"), 16)

                def step(g, load=True):
                    if load:
                        sp.wait_ge(stacks_loaded, (g + 3) * (16 * GIVES))
                        apart(sp, "sp")
                        sp.wait_ge(s2_done, 2 * HG * g)
                        apart(sp, "sp")
                        load_stacks(g + 3)
                    sp.wait_ge(sem(f"max_sent{l}"), (g + 1) * (16 * MP))
                    apart(sp, "sp")
                    send_maximum(g + 1)

                for b in range(B):
                    store_planes("k", b)
                for b in range(B):
                    store_planes("q", b)
                    if b == 0:
                        if l == 1:
                            sp.wait_ge(sem("down0_done"), T)
                        planes_left(sp, l, (B + b + 1) * C)
                        load_stacks(0)
                if l == 1:
                    for stack, rows in ((stack_q, a["rows_q"]), (stack_k, a["rows_k"])):
                        sp.dma_start(stack[KS:KS + MP + 1, :].rearrange("r (h t) -> r h t", t=S),
                                     rows[0:MP + 1].unsqueeze(1).broadcast_to([MP + 1, RING * HG, S])
                                     ).then_inc(sem("rows_back"), 16)
                for g in range(1, RING - 1):
                    sp.wait_ge(stacks_loaded, 16 * GIVES * g)
                    load_stacks(g)
                send_maximum(0)
                sp.wait_ge(stacks_loaded, 16 * GIVES * (RING - 1))
                load_stacks(RING - 1)
                sp.wait_ge(sem(f"max_sent{l}"), 16 * MP)
                send_maximum(1)
                planes_left(sp, l, 2 * B * C)
                sp.wait_ge(stacks_loaded, 16 * GIVES * RING)
                if l == 0:
                    sp.wait_ge(sem("vals_done0"), T // 2)
                    for s_ in "kvq":
                        sp.dma_start(w_qkv[s_][:], part(a[f"L1_W{s_}"])).then_inc(sem("w_layer1"), 16)
                if l == 1:
                    sp.wait_ge(sem("vals_done1"), T // 2)
                    sp.dma_start(w1_e_raw[:], a["L1_W1"].rearrange("e (c p) n -> p e c n", p=P)).then_inc(sem("w_moe"), 16)
                    for dst, src in ((w_mo_raw[:], part(a["L1_Wo"])), (w_router[:], part(a["L1_Wr"])),
                                     (bias_mo[:], a["L1_bo"].partition_broadcast(P)),
                                     (gamma[:], a["gamma"].partition_broadcast(P)), (beta[:], a["beta"].partition_broadcast(P))):
                        sp.dma_start(dst, src).then_inc(sem("w_moe"), 16)
                with sp.Fori(1, G - 3) as g:
                    step(g)
                step(G - 3, load=False)
                step(G - 2, load=False)
                if l == 0:
                    sp.wait_ge(sem("normalised0"), 2 * G)
                    sp.dma_start(w1_raw[:], part(a["L0_W1"])).then_inc(sem("w_ffn0"), 16)
                    sp.dma_start(w2_raw[:], part(a["L0_W2"])).then_inc(sem("w_ffn0"), 16)
            sp.wait_ge(sem("b1_cleared"), 1)
            for row in (0, 32):
                sp.dma_start(b1_raw[row:row + E, :], a["L1_b1"]).then_inc(sem("b1_loaded"), 16)
            for b in range(B - 1):
                sp.wait_ge(sem("x_final"), b + 1)
                sp.dma_start(out[b * S:(b + 1) * S, :].rearrange("(q p) d -> p q d", p=P), x[:, b * QT:(b + 1) * QT, :]
                             ).then_inc(sem("stored"), 16)
            for t in range((B - 1) * QT, T):
                sp.wait_ge(sem("x_final"), B + t - (B - 1) * QT)
                sp.dma_start(out[t * P:(t + 1) * P, :], x[:, t, :]).then_inc(sem("stored"), 16)
            sp.wait_ge(sem("stored"), 16 * (B - 1 + QT))

        @block.tensor
        def _(pe):
            mm, tr = nc.tensor.matmul, nc.tensor.transpose

            def project(l, s_, b, src):
                for c in range(C):
                    u = ((s_ == "q") * B + b) * C + c
                    wait(pe, sem(f"proj_high{l}"), u - 1)
                    for k in range(C):
                        last = mm(ps[u % 2][:], w_qkv[s_][:, k, c * P:(c + 1) * P],
                                  src[:, k, b * S:(b + 1) * S], start=(k == 0), stop=(k == C - 1))
                    last.then_inc(sem(f"proj_done{l}"), 1)

            def values(l, pairs=range(T // 2)):
                for v in pairs:
                    wait(pe, sem(f"vals_read{l}"), v - 3)
                    if l == 1:
                        wait(pe, sem("vals_high1"), v - 3)
                    for i in range(2):
                        t = 2 * v + i
                        for k in range(C):
                            last = mm(vals_bank(v)[:, i * D:(i + 1) * D], ctxT[:, k, t * P:(t + 1) * P], w_qkv["v"][:, k, :],
                                      start=(k == 0), stop=(k == C - 1))
                    last.then_inc(sem(f"vals_done{l}"), 1)

            def turn_project(l, between=lambda: None):
                name = f"n{2 * l}"
                for b in range(B + 1):
                    if b < B:
                        pe.wait_ge(sem(f"normed{2 * l}"), QT * (b + 1))
                        turn(name, b, sem(f"turned_read_{name}"))
                    if b == 0:
                        between()
                    else:
                        pe.wait_ge(sem(f"turned_read_{name}"), C * b)
                        project(l, "q", b - 1, xT)

            def turn(name, b, read):
                for c in range(C):
                    u = b * C + c
                    wait(pe, read, u - 3)
                    for i in range(QT):
                        last = tr(wide(u)[:, i * P:(i + 1) * P], xn[:, b * QT + i, c * P:(c + 1) * P], ident[:])
                    last.then_inc(sem(f"turned_{name}"), 1)

            def attention(l):
                s1_done, max_done = sem(f"s1_done{l}"), sem(f"max_done{l}")
                s2_done, exp_done = sem(f"scores_done{l}"), sem(f"exp_done{l}")
                pv_done, o_read = sem(f"pv_done{l}"), sem(f"o_read{l}")
                turned, sent = sem(f"max_turned{l}"), sem(f"max_sent{l}")
                rows = KS + (NR if l == 0 else MP + 1)

                def for_first_maximum(g, j):
                    for q in range(QT):
                        wait(pe, max_done, (g * HG + j - 1) * QT + q + 1)
                        mm(wide(q), stack_q[0:KS, slot(g, j) + q * P:slot(g, j) + (q + 1) * P],
                           stack_k[0:KS, slot(g, j):slot(g, j) + S], start=True, stop=True).then_inc(s1_done, 1)

                def for_maximum(g, r, j, tiles=range(QT)):
                    for q in tiles:
                        if j == 0 and q == 1:
                            wait(pe, sem(f"max_rest{l}"), g)
                        wait(pe, max_done, (g * HG + j) * QT + q - 1)
                        mm(ps[(q + 1) % 2][:], stack_q[0:KS, slot(r, j) + q * P:slot(r, j) + (q + 1) * P],
                           stack_k[0:KS, slot(r, j):slot(r, j) + S], start=True, stop=True).then_inc(s1_done, 1)

                def turn_maximum(g):
                    wait(pe, max_done, (g + 1) * HG * QT)
                    tr(ps[0][0:HG * QT, 0:P], row_max[:], ident[:]).then_inc(turned, 1)

                def scores(g, r, j, half):
                    if j == 0 and half == 0:
                        pe.wait_ge(sent, (g + 1) * (16 * MP))
                    wait(pe, exp_done, (g * HG + j) * 2 + half - 1)
                    for i in range(2):
                        k = 2 * half + i
                        last = mm(pw[half][:, i * S:(i + 1) * S], stack_k[0:rows, slot(r, j) + k * P:slot(r, j) + (k + 1) * P],
                                  stack_q[0:rows, slot(r, j):slot(r, j) + S], start=True, stop=(l == 1),
                                  skip_group_check=True)
                        if l == 0:
                            for p in range(2):
                                last = mm(pw[half][:, i * S + k * P:i * S + (k + 1) * P], rate_eye[:, p, :], behind[:],
                                          start=False, stop=(p == 1), skip_group_check=True)
                    last.then_inc(s2_done, 1)

                def weigh(g, j, tiles=range(QT)):
                    if 0 in tiles:
                        pe.wait_ge(exp_done, (g * HG + j) * 2 + 2)
                        lows_done(pe, l, g, 2 * j + 1)
                        if j % 2 == 0:
                            wait(pe, o_read, 2 * g + j // 2 - 1)
                    for q in tiles:
                        for k in range(QT):
                            for part_, probs_ in enumerate((probs_hi, probs_lo)):
                                last = mm(heads_out[j // 2][:, ((j % 2) * QT + q) * VW:((j % 2) * QT + q + 1) * VW],
                                          probs_[j][:, k * S + q * P:k * S + (q + 1) * P],
                                          vals[:, k, bass.ds(g * HG + j, 1), :],
                                          start=(k == 0 and part_ == 0), stop=(k == QT - 1 and part_ == 1))
                    if QT - 1 in tiles:
                        last.then_inc(pv_done, 1)

                def group(g, r, first=False, ahead=True, last=False):
                    for j in range(HG):
                        for half in range(2):
                            tiles = (2 * half, 2 * half + 1)
                            scores(g, r, j, half)
                            if j == 0 and half == 0 and not last:
                                turn_maximum(g + 1)
                            if ahead:
                                for_maximum(g + 2, (r + 2) % RING, j, tiles[:1])
                            if j >= LAG:
                                weigh(g, j - LAG, tiles)
                            elif not first:
                                weigh(g - 1, HG - LAG + j, tiles)
                            if ahead:
                                for_maximum(g + 2, (r + 2) % RING, j, tiles[1:])

                for g in range(2):
                    pe.wait_ge(sem(f"stacks_loaded{l}"), 16 * GIVES * (g + 1))
                    for j in range(HG):
                        for_first_maximum(g, j)
                    if g == 0:
                        turn_maximum(g)
                if l == 0:
                    pe.wait_ge(loaded_att, 16 * N_ATT)
                else:
                    pe.wait_ge(sem("rows_back"), 32)
                pe.wait_ge(sem(f"vals_low{l}"), T // 2)
                pe.wait_ge(sem(f"stacks_loaded{l}"), 16 * GIVES * 3)
                pe.wait_ge(max_done, 2 * HG * QT)
                group(0, 0, first=True)
                with pe.Fori(0, B - 1) as i:
                    for r in range(1, GB + 1):
                        g = GB * i + r
                        pe.wait_ge(sem(f"stacks_loaded{l}"), (g + 3) * (16 * GIVES))
                        group(g, r % RING)
                pe.wait_ge(sem(f"stacks_loaded{l}"), 16 * GIVES * G)
                group(G - 3, RING - 3)
                group(G - 2, RING - 2, ahead=False)
                group(G - 1, RING - 1, ahead=False, last=True)
                for j in range(HG - LAG, HG):
                    weigh(G - 1, j)

            pe.wait_ge(loaded_keys, 16 * N_KEYS)
            for b in range(B):
                project(0, "k", b, ctxT)
                if b == 0:
                    pe.wait_ge(loaded_values, 16 * N_VALUES)
                values(0, (2 * b, 2 * b + 1))
            pe.wait_ge(loaded_rows, 16 * N_ROWS)
            pe.wait_ge(sem("vals_read0"), T // 2)
            turn_project(0)
            pe.wait_ge(sem("rate_ready"), 3)
            pe.wait_ge(sem("proj_high0"), 2 * B * C)
            attention(0)

            def turn_n1(b):
                pe.wait_ge(sem("normed1"), QT * (b + 1))
                turn("n1", b, sem("rows0_lo"))

            pe.wait_ge(sem("exp_done0"), 2 * B * H)
            pe.wait_ge(sem("w_layer1"), 16 * 3)
            pe.wait_ge(sem("normalised0"), 2 * G)
            turn("att", 0, sem("turned_read_att"))
            for b in range(B):
                project(1, "k", b, ctxT)
                pe.wait_ge(sem("turned_read_att"), C * (b + 1))
                if b == 2:
                    pe.wait_ge(sem("q_step"), 1)
                for t in range(b * QT, (b + 1) * QT):
                    wait(pe, sem("oproj_tmp"), t - 1)
                    for k in range(C):
                        last = mm((po, pm)[t % 2][:, 0:D], xT[:, k, t * P:(t + 1) * P], w_o[:, k, :],
                                  start=(k == 0), stop=(k == C - 1))
                    last.then_inc(sem("oproj_done"), 1)
                wait(pe, sem("vals_high1"), 2 * b)
                if b < B - 1:
                    turn("att", b + 1, sem("turned_read_att"))
                else:
                    turn_n1(0)
                values(1, (2 * b, 2 * b + 1))
                if b == 1:
                    pe.wait_ge(sem("oproj_tmp"), QT * (b + 1))
                    for w in range(2):
                        pe.wait_ge(sem("abs_sum"), w + 1)
                        mm(pm[:, D + w:D + w + 1], ones[:], quant[:, w:w + 1], start=True, stop=True
                           ).then_inc(sem("gamma_done"), 1)

            def up0(b, f):
                u = b * FC + f
                wait(pe, sem("hid0_high"), u - 1)
                for k in range(C):
                    for h, rows in enumerate((xT_hi, xT_lo)):
                        last = mm(ps[u % 2][:], w1_q[:, k, f * P:(f + 1) * P], rows[:, b % 2, k, :],
                                  start=(k == 0 and h == 0), stop=(k == C - 1 and h == 1))
                last.then_inc(sem("up0_done"), 1)

            def down0(b, q):
                t = b * QT + q
                if t == 0:
                    pe.wait_ge(sem("w_quant"), 4)
                pe.wait_ge(sem("hid0_low"), (b + 1) * FC)
                wait(pe, sem("down0_tmp"), t - 1)
                for f in range(FC):
                    for h, rows in enumerate(PARTS):
                        last = mm((po, pm)[t % 2][:, 0:D], hid0[b % 2, rows][:, f, q * P:(q + 1) * P], w2_q[:, f, :],
                                  start=(f == 0 and h == 0), stop=(f == FC - 1 and h == 1))
                last.then_inc(sem("down0_done"), 1)

            pe.wait_ge(sem("vals_high1"), T // 2)
            pe.wait_ge(sem("w_quant"), 2)
            pe.wait_ge(sem("proj_high1"), B * C)
            for b in range(B):
                pe.wait_ge(sem("rows0_lo"), C * (b + 1))
                for f in range(FC):
                    up0(b, f)
                    if b > 0 and f % 2 == 1:
                        down0(b - 1, f // 2)
                    if f == 3 and b < B - 1:
                        turn_n1(b + 1)

            def last_block():
                for q in range(QT):
                    down0(B - 1, q)
                pe.wait_ge(sem("hid0_high"), B * FC)

            turn_project(1, last_block)
            pe.wait_ge(sem("proj_high1"), 2 * B * C)
            attention(1)

            def prepare(b, step):
                if step == 0:
                    pe.wait_ge(sem("normed3"), QT * (b + 1))
                    wait(pe, sem("masked_done"), 2 * E * b)
                    for c in range(C):
                        for i in range(QT):
                            last = tr(wide(c)[:, i * P:(i + 1) * P], xn[:, b * QT + i, c * P:(c + 1) * P], ident[:])
                        last.then_inc(sem("turned_n3"), 1)
                elif step == 1:
                    pe.wait_ge(sem("x3_ready"), C * (b + 1))
                    for q in range(QT):
                        for k in range(C):
                            last = mm(wide(2)[:, q * E:(q + 1) * E], x3[:, k, q * P:(q + 1) * P], w_router[:, k, :],
                                      start=(k == 0), stop=(k == C - 1))
                    last.then_inc(sem("logits_done"), 1)
                elif step == 2:
                    pe.wait_ge(sem("routed"), b + 1)
                    for q in range(QT):
                        last = tr(wide(3)[0:HOT, q * P:(q + 1) * P], onehot[:, q, :], ident[:])
                    last.then_inc(sem("hot_turned"), 1)
                else:
                    pe.wait_ge(sem("x3_low"), C * (b + 1))
                    pe.wait_ge(sem("hot_read"), b + 1)
                    for e in range(E):
                        mm(wide(e), select[0:E, e, :], onehotT[0:E, b % 2, :], start=True, stop=True).then_inc(sem("hot_spread"), 1)

            pe.wait_ge(sem("w_moe"), 16 * 6)
            pe.wait_ge(sem("exp_done1"), 2 * B * H)
            for step in range(3):
                prepare(0, step)
            pe.wait_ge(sem("select_ready"), E)
            prepare(0, 3)
            pe.wait_ge(sem("w1_high"), E)
            for b in range(B):
                for f in range(FC):
                    u = b * FC + f
                    wait(pe, sem("hid1_high"), u - 1)
                    for i, (r, w) in enumerate(PRODUCTS):
                        if u == 0 and w == 1:
                            pe.wait_ge(sem("w1_low"), len(LOWS_POOL))
                            pe.wait_ge(sem("w1_low_dve"), len(LOWS_DVE))
                        for e in range(E):
                            if f == 0 and w == 0:
                                pe.wait_ge(sem("masked_done"), (2 * b + r) * E + e + 1)
                            for c in range(C):
                                mm(ps[u % 2][:], w1_parts[w][:, e, c, f * P:(f + 1) * P], masked[r][:, e, c, :],
                                          start=(i == 0 and e == 0 and c == 0), stop=False)
                    if u == 0:
                        pe.wait_ge(sem("b1_split"), 1)
                    mm(ps[u % 2][:], b1_parts[0:HOT, f * P:(f + 1) * P], onehotT[0:HOT, b % 2, :], start=False, stop=True
                       ).then_inc(sem("up1_done"), 1)
                    if b < B - 1 and f in (2, 3, 4):
                        prepare(b + 1, f - 2)
                if b < B - 1:
                    prepare(b + 1, 3)
                if b == 0:
                    pe.wait_ge(sem("w_mo_low"), 1)
                pe.wait_ge(sem("hid1_low"), (b + 1) * FC)
                for q in range(QT):
                    t = b * QT + q
                    wait(pe, sem("down1_read"), t - 1)
                    for f in range(FC):
                        for i, (r, w) in enumerate(PRODUCTS):
                            last = mm((po, pm)[t % 2][:, 0:D], hid1[r][:, f, q * P:(q + 1) * P], w_mo_parts[w][:, f, :],
                                      start=(f == 0 and i == 0), stop=(f == FC - 1 and i == 2))
                    last.then_inc(sem("down1_done"), 1)

        @block.scalar
        def _(act):
            do = nc.scalar.activation

            def unit_out(l, u):
                query = u >= B * C
                act.wait_ge(sem(f"proj_done{l}"), u + 1)
                wait(act, sem(f"planes_kept{l}_{u % UNITS}"), 2 * 16 * (u // UNITS))
                if l == 0:
                    c = u % C
                    how = dict(func=ACT.Identity, bias=bias_qk[:, 2 if query else 1, c:c + 1], scale=0.25 if query else 1.0)
                else:
                    how = dict(func=ACT.Relu, scale=0.25 if query else 1.0)
                do(full[:, u % 2, :], ps[u % 2][:], **how)
                do(planes[:, u % UNITS, 0, :], ps[u % 2][:], **how).then_inc(sem(f"proj_high{l}"), 1)
                if u % (B * C) > 0:
                    middle(l, u - 1)
                if u % (B * C) == B * C - 1:
                    middle(l, u)

            def middle(l, u):
                act.wait_ge(sem(f"rest{l}"), u + 1)
                do(planes[:, u % UNITS, 1, :], rest[:, u % 2, :], ACT.Copy).then_inc(sem(f"middle{l}"), 1)

            def split_values(l, pairs=range(T // 2)):
                for i in pairs:
                    if l == 0:
                        act.wait_ge(sem(f"vals_read{l}"), i + 1)
                        do(vals_plane(i, 0), halves(v_full, i), ACT.Copy).then_inc(sem(f"vals_high{l}"), 1)
                    else:
                        act.wait_ge(sem(f"vals_done{l}"), i + 1)
                        do(v_full[:, i % VALS].rearrange("p n d -> p (n d)"), vals_bank(i), ACT.Relu).then_inc(sem(f"vals_read{l}"), 1)
                        do(vals_plane(i, 0), vals_bank(i).rearrange("p (n h d) -> p n h d", n=2, d=DH), ACT.Relu
                           ).then_inc(sem(f"vals_high{l}"), 1)
                    if i > 0:
                        middle_values(l, i - 1)
                if i == T // 2 - 1:
                    middle_values(l, i)

            def middle_values(l, i):
                act.wait_ge(sem(f"vals_rest{l}"), i + 1)
                do(vals_plane(i, 1), halves(v_rest, i), ACT.Copy).then_inc(sem(f"vals_middle{l}"), 1)

            def queries_out(l):
                for b in range(B + 1):
                    if b < B:
                        turned_out(f"n{2 * l}", b)
                    if b > 0:
                        for c in range(C):
                            unit_out(l, (B + b - 1) * C + c)

            def turned_out(name, b):
                for c in range(C):
                    u = b * C + c
                    act.wait_ge(sem(f"turned_{name}"), u + 1)
                    do(xT[:, c, b * S:(b + 1) * S], wide(u), ACT.Copy).then_inc(sem(f"turned_read_{name}"), 1)

            def attention(l):
                s2_done, exp_done, pv_done = sem(f"scores_done{l}"), sem(f"exp_done{l}"), sem(f"pv_done{l}")
                turned = sem(f"max_turned{l}")

                def high_maximum(g):
                    act.wait_ge(turned, g + 1)
                    wait(act, sem(f"max_sent{l}"), g * (16 * MP))
                    do(max_planes[0:HG * QT, 0, :], ps[0][0:HG * QT, 0:P], ACT.Copy, scale=-1.0
                       ).then_inc(sem(f"max_high{l}"), 1)

                def group(g, last=False):
                    if not last:
                        high_maximum(g + 1)
                    for j in range(HG):
                        for half in range(2):
                            n = (g * HG + j) * 2 + half
                            act.wait_ge(s2_done, n + 1)
                            if half == 0:
                                wait(act, pv_done, (g - 1) * HG + j + 1)
                                lows_done(act, l, g, 2 * j - 3)
                            cols = slice(half * 2 * S, (half + 1) * 2 * S)
                            do(probs[j % 2][:, cols], pw[half][:], ACT.Exp)
                            do(probs_hi[j][:, cols], pw[half][:], ACT.Exp).then_inc(exp_done, 1)

                high_maximum(0)
                planes_left(act, l, 2 * B * C)
                act.wait_ge(sem(f"vals_low{l}"), T // 2)
                group(0)
                with act.Fori(0, G // 2 - 1) as i:
                    group(2 * i + 1)
                    group(2 * i + 2)
                group(G - 1, last=True)

            act.wait_ge(sem("prepared"), 1)
            for b in range(B):
                for c in range(C):
                    unit_out(0, b * C + c)
                split_values(0, (2 * b, 2 * b + 1))
            queries_out(0)
            act.wait_ge(loaded_rest, 16 * N_REST)
            do(gates[:], gates_raw[:], ACT.Tanh).then_inc(sem("gates"), 1)
            attention(0)

            act.wait_ge(sem("normalised0"), 2 * G)
            def rows0_high(b):
                act.wait_ge(sem("oproj_done"), T)
                wait(act, sem("up0_done"), (b - 1) * FC)
                for c in range(C):
                    act.wait_ge(sem("turned_n1"), b * C + c + 1)
                    do(xT_hi[:, b % 2, c, :], wide(b * C + c), ACT.Copy).then_inc(sem("rows0_hi"), 1)

            turned_out("att", 0)
            for b in range(B):
                for c in range(C):
                    unit_out(1, b * C + c)
                if b < 2:
                    act.wait_ge(sem("w_ffn0"), 32)
                    wait(act, sem("abs_sum"), b)
                    do(w_abs[:], (w1_raw, w2_raw)[b][:].rearrange("p c n -> p (c n)"), ACT.Abs,
                       accum_out=quant[:, b:b + 1]).then_inc(sem("abs_sum"), 1)
                if b < B - 1:
                    turned_out("att", b + 1)
                else:
                    rows0_high(0)
                split_values(1, (2 * b, 2 * b + 1))

            planes_left(act, 1, B * C)
            act.wait_ge(sem("vals_low1"), T // 2)
            for b in range(B):
                wait(act, sem("down0_done"), QT * (b - 1))
                for f in range(FC):
                    u = b * FC + f
                    act.wait_ge(sem("up0_done"), u + 1)
                    wait(act, sem("hid0_low"), u - 3)
                    do(hid0_full[:, u % 4, :], ps[u % 2][:], ACT.Relu, bias=b1_cols[:, f:f + 1])
                    do(hid0[b % 2, "hi"][:, f, :], ps[u % 2][:], ACT.Relu, bias=b1_cols[:, f:f + 1]).then_inc(sem("hid0_high"), 1)
                    if f == 3 and b < B - 1:
                        rows0_high(b + 1)
            act.wait_ge(sem("down0_done"), QT * (B - 1))
            queries_out(1)
            act.wait_ge(sem("down0_done"), T)
            attention(1)

            def weights_high(e):
                do(w1_parts[0][:, e], w1_e_raw[:, e], ACT.Copy).then_inc(sem("w1_high"), 1)

            act.wait_ge(sem("w_moe"), 16 * 6)
            act.wait_ge(sem("scores_done1"), 2 * B * H)
            for e in LOWS_POOL:
                weights_high(e)
            act.wait_ge(sem("normalised1"), 2 * G)

            def rows1(b):
                for c in range(C):
                    act.wait_ge(sem("turned_n3"), b * C + c + 1)
                    do(x3[:, c, :], wide(c), ACT.Copy).then_inc(sem("x3_ready"), 1)
                    do(x3_parts[0][:, c, :], wide(c), ACT.Copy).then_inc(sem("x3_high"), 1)

            weights_high(0)
            rows1(0)
            weights_high(1)
            act.wait_ge(sem("b1_loaded"), 32)
            do(b1_parts[0:HOT, :], b1_raw[0:HOT, :], ACT.Copy).then_inc(sem("b1_high"), 1)
            do(w_mo_parts[0][:], w_mo_raw[:], ACT.Copy).then_inc(sem("w_mo_high"), 1)
            for b in range(B):
                wait(act, sem("down1_done"), QT * b)
                for f in range(FC):
                    u = b * FC + f
                    act.wait_ge(sem("up1_done"), u + 1)
                    wait(act, sem("hid1_low"), u - 1)
                    do(hid1_full[:, u % 2, :], ps[u % 2][:], ACT.Gelu)
                    do(hid1[0][:, f, :], ps[u % 2][:], ACT.Gelu).then_inc(sem("hid1_high"), 1)
                    if b < B - 1 and f == 2:
                        rows1(b + 1)

        @block.gpsimd
        def _(pool):
            nc.gpsimd.memset(minus_half[:], -0.5).then_inc(sem("half_ready"), 1)
            pool.wait_ge(sem("half_ready"), 1)
            v = nc.gpsimd

            def roots(n, b, q=None):
                pool.wait_ge(sem("var_ready"), n * B + b + (q or 0) + 1)
                ts = slice(b * QT, (b + 1) * QT) if q is None else slice(b * QT + q, b * QT + q + 1)
                v.tensor_tensor(root[:, ts], var_eps[:, ts], minus_half[:, ts], ALU.pow).then_inc(sem("root_ready"), 1)

            def split_values(l, pairs=range(T // 2)):
                for i in pairs:
                    pool.wait_ge(sem(f"vals_high{l}"), i + 1)
                    wait(pool, sem(f"vals_low{l}"), i - 1)
                    v.tensor_tensor(halves(v_rest, i), halves(v_full, i), vals_plane(i, 0), ALU.subtract
                                    ).then_inc(sem(f"vals_rest{l}"), 1)
                    if i > 0:
                        low_values(l, i - 1)
                if i == T // 2 - 1:
                    low_values(l, i)

            def low_values(l, i):
                pool.wait_ge(sem(f"vals_middle{l}"), i + 1)
                v.tensor_tensor(vals_plane(i, 2), halves(v_rest, i), vals_plane(i, 1), ALU.subtract
                                ).then_inc(sem(f"vals_low{l}"), 1)

            def split(l, s_, b):
                for c in range(C):
                    u = ((s_ == "q") * B + b) * C + c
                    pool.wait_ge(sem(f"proj_high{l}"), u + 1)
                    wait(pool, sem(f"planes_ready{l}"), u - 1)
                    v.tensor_tensor(rest[:, u % 2, :], full[:, u % 2, :], planes[:, u % UNITS, 0, :],
                                    ALU.subtract).then_inc(sem(f"rest{l}"), 1)
                    if u % (B * C) > 0:
                        low_plane(l, u - 1)
                    if u % (B * C) == B * C - 1:
                        low_plane(l, u)

            def low_plane(l, u):
                pool.wait_ge(sem(f"middle{l}"), u + 1)
                v.tensor_tensor(planes[:, u % UNITS, 2, :], rest[:, u % 2, :], planes[:, u % UNITS, 1, :],
                                ALU.subtract).then_inc(sem(f"planes_ready{l}"), 1)

            def attention(l):
                def low_maximum(g):
                    n = HG * QT
                    pool.wait_ge(sem(f"max_rest{l}"), g + 1)
                    apart(pool, "pool")
                    v.tensor_copy(max_planes[0:n, 1, :], max_rest[0:n, :]).then_inc(sem(f"max_middle{l}"), 1)
                    pool.wait_ge(sem(f"max_middle{l}"), g + 1)
                    v.tensor_tensor(max_planes[0:n, 2, :], max_rest[0:n, :], max_planes[0:n, 1, :], ALU.subtract
                                    ).then_inc(sem(f"max_split{l}"), 1)

                def group(g, last=False):
                    for n in LOW_POOL:
                        low_part(pool, v, l, g, n).then_inc(sem(f"low_pool{l}"), 1)
                        if n == LOW_POOL[1] and not last:
                            low_maximum(g + 1)

                low_maximum(0)
                group(0)
                with pool.Fori(0, G // 2 - 1) as i:
                    group(2 * i + 1)
                    group(2 * i + 2)
                if l == 1:
                    roots(3, 0)
                group(G - 1, last=True)
                if l == 1:
                    for b in range(1, B - 1):
                        roots(3, b)

            for b in range(B):
                split_values(0, (2 * b, 2 * b + 1))
                roots(0, b)
            for u in range(B * C, 2 * B * C):
                low_plane(0, u)
            attention(0)
            for b in range(B):
                split(1, "k", b)
                roots(1, b)
                split_values(1, (2 * b, 2 * b + 1))
            planes_left(pool, 1, B * C)
            for b in range(B):
                for f in range(FC):
                    u = b * FC + f
                    pool.wait_ge(sem("hid0_high"), u + 1)
                    v.tensor_tensor(hid0[b % 2, "lo"][:, f, :], hid0_full[:, u % 4, :], hid0[b % 2, "hi"][:, f, :], ALU.subtract
                                    ).then_inc(sem("hid0_low"), 1)
                    if b >= 2 and f == 1:
                        roots(2, b - 2)
            roots(2, B - 2)
            roots(2, B - 1)
            for u in range(B * C, 2 * B * C):
                low_plane(1, u)
            attention(1)

            pool.wait_ge(sem("normalised1"), 2 * G)
            for i, e in enumerate(LOWS_POOL):
                pool.wait_ge(sem("w1_high"), i + 1)
                v.tensor_tensor(w1_parts[1][:, e], w1_e_raw[:, e], w1_parts[0][:, e], ALU.subtract).then_inc(sem("w1_low"), 1)
            pool.wait_ge(sem("w_mo_high"), 1)
            v.tensor_tensor(w_mo_parts[1][:], w_mo_raw[:], w_mo_parts[0][:], ALU.subtract).then_inc(sem("w_mo_low"), 1)
            roots(3, B - 1)
            for b in range(B):
                for f in range(FC):
                    u = b * FC + f
                    pool.wait_ge(sem("hid1_high"), u + 1)
                    v.tensor_tensor(hid1[1][:, f, :], hid1_full[:, u % 2, :], hid1[0][:, f, :], ALU.subtract
                                    ).then_inc(sem("hid1_low"), 1)
                    if b > 0 and f == 3:
                        roots(4, b - 1)
            for q in range(QT):
                roots(4, B - 1, q)

        @block.vector
        def _(dve):
            v = nc.vector

            def tiles(b, q):
                return range(b * QT, (b + 1) * QT) if q is None else range(b * QT + q, b * QT + q + 1)

            def variance(n, b, src, eps, q=None):
                ts = tiles(b, q)
                for t in ts:
                    v.bn_stats(stats[:, t, :], src[:, t, :]).then_inc(sem(f"stats{n}"), 1)
                dve.wait_ge(sem(f"stats{n}"), ts[-1] + 1)
                for t in ts:
                    v.bn_aggr(meanvar[:, t, :], stats[:, t, :]).then_inc(sem(f"aggr{n}"), 1)
                dve.wait_ge(sem(f"aggr{n}"), ts[-1] + 1)
                v.tensor_scalar(var_eps[:, ts[0]:ts[-1] + 1], meanvar[:, ts[0]:ts[-1] + 1, 1], eps, None, ALU.add
                                ).then_inc(sem("var_ready"), 1)

            def normal(n, b, src, q=None):
                ts = tiles(b, q)
                w, r, h, y1 = (z[:, ts[0]:ts[-1] + 1] for z in (var_eps, root, newton, rstd))
                st, k = sem("newton_step"), 4 * (n * B + b + (q or 0))
                dve.wait_ge(sem("root_ready"), k // 4 + 1)
                v.tensor_tensor(h, r, r, ALU.mult).then_inc(st, 1)
                dve.wait_ge(st, k + 1)
                v.tensor_tensor(h, h, w, ALU.mult).then_inc(st, 1)
                dve.wait_ge(st, k + 2)
                v.tensor_scalar(h, h, -0.5, 1.5, ALU.mult, ALU.add).then_inc(st, 1)
                dve.wait_ge(st, k + 3)
                v.tensor_tensor(y1, h, r, ALU.mult).then_inc(st, 1)
                dve.wait_ge(st, k + 4)
                for t in ts:
                    v.tensor_scalar(xn[:, t, :], src[:, t, :], meanvar[:, t, 0:1], rstd[:, t:t + 1],
                                    ALU.subtract, ALU.mult).then_inc(sem(f"normed{n}"), 1)

            def split(l, s_, b):
                for c in range(C):
                    u = ((s_ == "q") * B + b) * C + c
                    dve.wait_ge(sem(f"proj_high{l}"), u + 1)
                    wait(dve, sem(f"planes_ready{l}"), u - 1)
                    v.tensor_tensor(rest[:, u % 2, :], full[:, u % 2, :], planes[:, u % UNITS, 0, :],
                                    ALU.subtract).then_inc(sem(f"rest{l}"), 1)
                    if s_ == "k":
                        if u > 0:
                            low_plane(l, u - 1)
                        if u == B * C - 1:
                            low_plane(l, u)

            def low_plane(l, u):
                dve.wait_ge(sem(f"middle{l}"), u + 1)
                v.tensor_tensor(planes[:, u % UNITS, 2, :], rest[:, u % 2, :], planes[:, u % UNITS, 1, :],
                                ALU.subtract).then_inc(sem(f"planes_ready{l}"), 1)

            def values0(k):
                dve.wait_ge(sem("vals_done0"), k + 1)
                wait(dve, sem("vals_rest0"), k - VALS + 1)
                v.tensor_tensor(v_full[:, k % VALS], vals_bank(k).rearrange("p (n d) -> p n d", n=2),
                                bias_v[:].unsqueeze(1).broadcast_to([P, 2, D]), ALU.add).then_inc(sem("vals_read0"), 1)

            def variance3(b):
                for t in range(b * QT, (b + 1) * QT):
                    v.scalar_tensor_tensor(out=x[:, t, :], in0=xn[:, t, :], scalar=gates[:, 1:2], in1=x[:, t, :],
                                           op0=ALU.mult, op1=ALU.add).then_inc(sem("x_att1"), 1)
                dve.wait_ge(sem("x_att1"), QT * (b + 1))
                variance(3, b, x, 1e-5)

            def attention(l):
                s1_done, max_done = sem(f"s1_done{l}"), sem(f"max_done{l}")
                pv_done, o_read, turned = sem(f"pv_done{l}"), sem(f"o_read{l}"), sem(f"max_turned{l}")

                def maxima(g, j, first=False):
                    if j == 0:
                        wait(dve, turned, g)
                    for q in range(QT):
                        dst = row_max[:, j * QT + q:j * QT + q + 1]
                        bank = wide(q) if first else ps[(q + 1) % 2][:]
                        dve.wait_ge(s1_done, (g * HG + j) * QT + q + 1)
                        if first:
                            wait(dve, max_done, (g * HG + j) * QT + q - 1)
                        if l == 0:
                            apart(dve, "dve")
                            at = (QT - 1 - q) * P
                            v.tensor_tensor_reduce(biased[:, q % 2, :], bank, time_bias[:, at:at + S], 1.0, LOWEST,
                                                   ALU.add, ALU.max, dst).then_inc(max_done, 1)
                        else:
                            v.tensor_reduce(dst, bank, AX, ALU.max).then_inc(max_done, 1)

                def rest_maximum(g):
                    n = HG * QT
                    dve.wait_ge(sem(f"max_high{l}"), g + 1)
                    wait(dve, sem(f"max_split{l}"), g)
                    v.scalar_tensor_tensor(out=max_rest[0:n, :], in0=ps[0][0:n, 0:P], scalar=-1.0, in1=max_planes[0:n, 0, :],
                                           op0=ALU.mult, op1=ALU.subtract).then_inc(sem(f"max_rest{l}"), 1)

                def normalise(g, b, n, i):
                    dve.wait_ge(pv_done, g * HG + 2 * i + 2)
                    wait(dve, sem(f"normalised{l}"), 2 * g + i)
                    o = heads_out[i][:, 0:2 * QT * VW].rearrange("p (n w) -> p n w", w=VW)
                    v.reciprocal(recip[:], o[:, :, VP * DH]).then_inc(sem(f"recip{l}"), 1)
                    planes_last = o[:, :, 0:VP * DH].rearrange("p n (v d) -> p n d v", v=VP)
                    v.tensor_reduce(summed[:], planes_last, AX, ALU.add).then_inc(o_read, 1)
                    dve.wait_ge(sem(f"recip{l}"), 2 * g + i + 1)
                    dve.wait_ge(o_read, 2 * g + i + 1)
                    by_pair = xn[:].rearrange("p (b q) (n i j d) -> p b n i q j d", q=QT, n=GB, i=2, d=DH)
                    dst = by_pair[:, bass.ds(b, 1), n, i].rearrange("p b q j d -> p (b q) j d")
                    v.tensor_tensor(dst, summed[:].rearrange("p (j q) d -> p q j d", q=QT),
                                    recip[:].rearrange("p (j q) -> p q j", q=QT).unsqueeze(3).broadcast_to([P, QT, 2, DH]),
                                    ALU.mult).then_inc(sem(f"normalised{l}"), 1)

                def group(g, before=None, ahead=True, last=False):
                    if not last:
                        rest_maximum(g + 1)
                    for j in range(HG):
                        if ahead:
                            maxima(g + 2, j)
                        for n in LOW_DVE:
                            if n // 2 == j:
                                low_part(dve, v, l, g, n).then_inc(sem(f"low_dve{l}"), 1)
                        if j % 2 == 0 and before is not None:
                            normalise(g - 1, *before, j // 2)

                for g in range(2):
                    for j in range(HG):
                        maxima(g, j, first=True)
                    if g == 0:
                        rest_maximum(g)
                group(0)
                with dve.Fori(0, B - 1) as b:
                    for n in range(GB):
                        group(GB * b + n + 1, (b, n))
                group(G - 3, (B - 1, GB - 4))
                if l == 1:
                    variance3(0)
                group(G - 2, (B - 1, GB - 3), ahead=False)
                if l == 1:
                    variance3(1)
                    variance3(2)
                group(G - 1, (B - 1, GB - 2), ahead=False, last=True)
                for i in range(2):
                    normalise(G - 1, B - 1, GB - 1, i)
                dve.wait_ge(sem(f"normalised{l}"), 2 * G)

            def thresholds():
                dve.wait_ge(sem("gamma_done"), 2)
                v.tensor_scalar(quant[:, 2:4], pm[:, D:D + 2], 1.0 / (D * FF), 1e-5, ALU.mult, ALU.add).then_inc(sem("q_step"), 1)
                dve.wait_ge(sem("q_step"), 1)
                v.tensor_scalar(quant[:, 4:6], quant[:, 2:4], 0.5, None, ALU.mult).then_inc(sem("q_step"), 1)
                v.tensor_scalar(quant[:, 6:8], quant[:, 2:4], -0.5, None, ALU.mult).then_inc(sem("q_step"), 1)

            def quantise(w):
                dve.wait_ge(sem("q_step"), 3)
                raw, q = ((w1_raw, w1_q), (w2_raw, w2_q))[w]
                v.tensor_scalar(q[:], raw[:], quant[:, 6 + w:7 + w], None, ALU.is_lt).then_inc(sem("w_quant"), 1)
                dve.wait_ge(sem("w_quant"), 2 * w + 1)
                v.scalar_tensor_tensor(out=q[:], in0=raw[:], scalar=quant[:, 4 + w:5 + w], in1=q[:],
                                       op0=ALU.is_gt, op1=ALU.subtract).then_inc(sem("w_quant"), 1)

            def add_gated(step, t, bias, gate):
                dve.wait_ge(sem(f"{step}_done"), t + 1)
                v.tensor_tensor(tmp[:, t % 2, :], (po, pm)[t % 2][:, 0:D], bias, ALU.add).then_inc(sem(f"{step}_tmp"), 1)
                dve.wait_ge(sem(f"{step}_tmp"), t + 1)
                v.scalar_tensor_tensor(out=x[:, t, :], in0=tmp[:, t % 2, :], scalar=gates[:, gate:gate + 1],
                                       in1=x[:, t, :], op0=ALU.mult, op1=ALU.add).then_inc(sem(f"{step}_added"), 1)

            v.memset(ones[:], 1.0).then_inc(sem("dve_const"), 1)
            v.memset(vals[:, :, :, VP * DH:VW], 1.0).then_inc(sem("dve_const"), 1)
            v.memset(onehot[:], 0.0).then_inc(sem("dve_const"), 1)
            dve.wait_ge(loaded_keys, 16 * N_KEYS)
            v.tensor_scalar(bias_qk[:, 2, :], bias_qk[:, 0, :], 0.25, None, ALU.mult).then_inc(sem("prepared"), 1)
            for b in range(B):
                split(0, "k", b)
                if b == 0:
                    dve.wait_ge(loaded_values, 16 * N_VALUES)
                for k in (2 * b, 2 * b + 1):
                    values0(k)
                if b == 0:
                    dve.wait_ge(loaded_rows, 16 * N_ROWS)
                variance(0, b, x, 1e-5)
                if b > 0:
                    normal(0, b - 1, x)
            normal(0, B - 1, x)
            dve.wait_ge(loaded_rest, 16 * N_REST)
            v.tensor_copy(behind[:], behind_raw[:]).then_inc(sem("rate_ready"), 1)
            v.tensor_scalar(rate_eye[:, 0, :], ident[:], float(TIME_RATE), None, ALU.mult).then_inc(sem("rate_ready"), 1)
            dve.wait_ge(sem("rate_ready"), 2)
            v.scalar_tensor_tensor(out=rate_eye[:, 1, :], in0=ident[:], scalar=float(TIME_RATE), in1=rate_eye[:, 0, :],
                                   op0=ALU.mult, op1=ALU.subtract).then_inc(sem("rate_ready"), 1)
            dve.wait_ge(sem("rate_ready"), 3)

            for b in range(B):
                split(0, "q", b)
            attention(0)

            dve.wait_ge(sem("gates"), 1)
            def rows0_low(b):
                wait(dve, sem("up0_done"), (b - 1) * FC)
                for c in range(C):
                    u = b * C + c
                    dve.wait_ge(sem("rows0_hi"), u + 1)
                    v.tensor_tensor(xT_lo[:, b % 2, c, :], wide(u), xT_hi[:, b % 2, c, :], ALU.subtract
                                    ).then_inc(sem("rows0_lo"), 1)

            for b in range(B):
                for t in range(b * QT, (b + 1) * QT):
                    add_gated("oproj", t, bias_o[:], 0)
                dve.wait_ge(sem("oproj_added"), QT * (b + 1))
                variance(1, b, x, 1e-5)
                if b == 1:
                    thresholds()
                elif b == 2:
                    quantise(0)
                elif b == 3:
                    rows0_low(0)
                dve.wait_ge(sem("turned_att"), C * (b + 1))
                normal(1, b, x)
            quantise(1)

            def variance2(b):
                dve.wait_ge(sem("down0_added"), QT * (b + 1))
                variance(2, b, x, 1e-5)

            def normal2(b):
                dve.wait_ge(sem("turned_n1"), C * (b + 1))
                normal(2, b, x)

            rows0_low(1)
            for b in range(B):
                for q in range(QT):
                    add_gated("down0", b * QT + q, bias_2[:], 2)
                    if q == 1:
                        if b > 0:
                            normal2(b - 1)
                        if b + 2 < B:
                            rows0_low(b + 2)
                variance2(b)
            split(1, "q", 0)
            normal2(B - 1)
            for b in range(1, B):
                split(1, "q", b)
            attention(1)

            def route(b):
                rt, k = sem("route_step"), 4 * b
                dve.wait_ge(sem("logits_done"), b + 1)
                v.tensor_copy(logits[:], wide(2)[:, 0:QT * E].rearrange("p (t e) -> p t e", e=E)).then_inc(sem("logits_read"), 1)
                dve.wait_ge(sem("logits_read"), b + 1)
                v.tensor_reduce(top[:], logits[:], AX, ALU.max).then_inc(rt, 1)
                dve.wait_ge(rt, k + 1)
                wait(dve, sem("hot_turned"), b)
                v.tensor_tensor(onehot[:, :, 0:E], logits[:], top[:].unsqueeze(2).broadcast_to([P, QT, E]), ALU.is_equal
                                ).then_inc(rt, 1)
                dve.wait_ge(rt, k + 2)
                v.tensor_tensor(logits[:], onehot[:, :, 0:E], order[:].unsqueeze(1).broadcast_to([P, QT, E]), ALU.mult
                                ).then_inc(rt, 1)
                dve.wait_ge(rt, k + 3)
                v.tensor_reduce(top[:], logits[:], AX, ALU.max).then_inc(rt, 1)
                dve.wait_ge(rt, k + 4)
                for i in range(2):
                    ins = v.tensor_tensor(onehot[:, :, 32 * i:32 * i + E], logits[:], top[:].unsqueeze(2).broadcast_to([P, QT, E]),
                                          ALU.is_equal)
                ins.then_inc(sem("routed"), 1)
                dve.wait_ge(sem("hot_turned"), b + 1)
                v.tensor_copy(onehotT[0:HOT, b % 2, :], wide(3)[0:HOT, :]).then_inc(sem("hot_read"), 1)

            def rows_low(b):
                for c in range(C):
                    dve.wait_ge(sem("x3_high"), b * C + c + 1)
                    v.tensor_tensor(x3_parts[1][:, c, :], wide(c), x3_parts[0][:, c, :], ALU.subtract).then_inc(sem("x3_low"), 1)

            def mask(b, h, e):
                if e == 0 and h == 0:
                    wait(dve, sem("up1_done"), FC * b)
                if h == 0:
                    dve.wait_ge(sem("hot_spread"), b * E + e + 1)
                if e == 0 and h == 1:
                    dve.wait_ge(sem("x3_low"), C * (b + 1))
                v.tensor_tensor(masked[h][:, e], x3_parts[h][:], wide(e).unsqueeze(1).broadcast_to([P, C, S]), ALU.mult
                                ).then_inc(sem("masked_done"), 1)

            def residual(t):
                dve.wait_ge(sem("down1_done"), t + 1)
                v.tensor_tensor(xn[:, t, :], (po, pm)[t % 2][:, 0:D], xn[:, t, :], ALU.add).then_inc(sem("down1_read"), 1)
                dve.wait_ge(sem("down1_read"), t + 1)
                v.tensor_tensor(xn[:, t, :], xn[:, t, :], bias_mo[:], ALU.add).then_inc(sem("biased_out"), 1)

            def finish(b, q=None):
                normal(4, b, xn, q)
                ts = tiles(b, q)
                dve.wait_ge(sem("normed4"), ts[-1] + 1)
                rows = xn[:, ts[0]:ts[-1] + 1, :]
                for i, (by, op) in enumerate(((gamma, ALU.mult), (beta, ALU.add))):
                    v.tensor_tensor(rows, rows, by[:].unsqueeze(1).broadcast_to([P, len(ts), D]), op).then_inc(sem("scaled"), 1)
                    dve.wait_ge(sem("scaled"), 2 * (b + (q or 0)) + i + 1)
                xb = x[:, ts[0]:ts[-1] + 1, :]
                v.scalar_tensor_tensor(out=xb, in0=rows, scalar=gates[:, 3:4], in1=xb, op0=ALU.mult, op1=ALU.add
                                       ).then_inc(sem("x_final"), 1)

            def variance4(b, q=None):
                dve.wait_ge(sem("biased_out"), tiles(b, q)[-1] + 1)
                variance(4, b, xn, 1e-12, q)

            def weights_low(e):
                dve.wait_ge(sem("w1_high"), len(LOWS_POOL) + LOWS_DVE.index(e) + 1)
                v.tensor_tensor(w1_parts[1][:, e], w1_e_raw[:, e], w1_parts[0][:, e], ALU.subtract).then_inc(sem("w1_low_dve"), 1)

            normal(3, 0, x)
            weights_low(0)
            dve.wait_ge(sem("w1_low_dve"), 1)
            rows_low(0)
            v.memset(b1_raw[0:HOT, :], 0.0).then_inc(sem("b1_cleared"), 1)
            for e in range(E):
                v.tensor_copy(select[0:E, e, :], ident[0:E, e:e + 1].broadcast_to([E, P])).then_inc(sem("select_ready"), 1)
            weights_low(1)
            route(0)
            dve.wait_ge(sem("w1_low_dve"), len(LOWS_DVE))
            dve.wait_ge(sem("w1_low"), 1)
            for b in range(B):
                for h in range(2):
                    for e in range(E):
                        if b == 0 and (h, e) == (1, 1):
                            dve.wait_ge(sem("b1_high"), 1)
                            v.tensor_tensor(b1_parts[32:HOT, :], b1_raw[32:HOT, :], b1_parts[32:HOT, :], ALU.subtract
                                            ).then_inc(sem("b1_split"), 1)
                        if b == 0 and (h, e) == (1, 0):
                            dve.wait_ge(sem("w_mo_low"), 1)
                        mask(b, h, e)
                        if b > 0 and e % 2 == 1:
                            residual((b - 1) * QT + 2 * h + e // 2)
                if b == 0:
                    normal(3, 1, x)
                    normal(3, 2, x)
                    variance3(B - 1)
                    normal(3, B - 1, x)
                else:
                    variance4(b - 1)
                if b < B - 1:
                    rows_low(b + 1)
                    route(b + 1)
                if b > 0:
                    finish(b - 1)
            for q in range(QT + 1):
                if q < QT:
                    residual((B - 1) * QT + q)
                    variance4(B - 1, q)
                if q > 0:
                    finish(B - 1, q - 1)


def kernel(**inputs):
    import concourse.bacc as _bacc
    from concourse.bass_utils import run_bass_kernel_spmd as _run

    def host(name):
        return np.asarray(inputs[name])

    def cols(v):
        return v.reshape(-1, P).T

    def grouped(v):
        return v.reshape(GB, HG, DH, -1).transpose(0, 2, 1, 3).reshape(v.shape)

    lay = {
        "x": host("x").reshape(B * S, D), "ctxT": host("ctx_1024").reshape(B * S, D).T,
        "gates": np.concatenate([host("g_xattn"), host("g_ffn")]),
        "L0_Wq": grouped(host("L0_xattn_Wq")).T, "L0_Wk": grouped(host("L0_xattn_Wk")).T, "L0_Wv": host("L0_xattn_Wv").T,
        "L0_Wo": host("L0_xattn_Wo").T, "L0_bq": cols(grouped(host("L0_xattn_bq"))), "L0_bk": cols(grouped(host("L0_xattn_bk"))),
        "L0_bv": host("L0_xattn_bv"), "L0_bo": host("L0_xattn_bo"),
        "L0_W1": host("L0_ffn_W1").T, "L0_b1": cols(host("L0_ffn_b1")), "L0_W2": host("L0_ffn_W2").T,
        "L0_b2": host("L0_ffn_b2"),
        "L1_Wq": grouped(host("L1_xattn_Wq")).T, "L1_Wk": grouped(host("L1_xattn_Wk")).T, "L1_Wv": host("L1_xattn_Wv").T,
        "L1_Wr": host("L1_ffn_W_router"), "L1_W1": host("L1_ffn_W1"), "L1_b1": host("L1_ffn_b1"),
        "L1_Wo": host("L1_ffn_Wo"), "L1_bo": host("L1_ffn_bo"), "gamma": host("L1_ffn_ln_gamma"),
        "beta": host("L1_ffn_ln_beta"),
    }
    import ml_dtypes
    tables = constants()
    for name in ("rows_q", "rows_k"):
        tables[name] = tables[name].astype(ml_dtypes.bfloat16)
    lay.update(tables)
    nc = _bacc.Bacc("TRN2", target_bir_lowering=False, num_devices=1)
    arrays, args = {}, {}
    for name, v in lay.items():
        v = np.ascontiguousarray(v)
        arrays[f"in_{name}"] = v
        args[name] = nc.dram_tensor(f"in_{name}", v.shape, mybir.dt.from_np(v.dtype), kind="ExternalInput").ap()
    out = nc.dram_tensor("out_x", (B * S, D), F32, kind="ExternalOutput").ap()
    gated_blocks_program(nc, args, out)
    r = _run(nc, [arrays], core_ids=[0])
    return r.results[0]["out_x"].reshape(B, S, D)
```
